# Optimizing a Trainium2 kernel written in Bass

```python
import numpy as np
import jax
import jax.numpy as jnp

def _softmax(x, axis=-1):
    return jax.nn.softmax(x, axis=axis)

def _gelu(x):
    return jax.nn.gelu(x, approximate=True)

def _silu(x):
    return jax.nn.silu(x)

def _sigmoid(x):
    return jax.nn.sigmoid(x)

def _layernorm(x, axis=-1, eps=1e-05):
    m = jnp.mean(x, axis=axis, keepdims=True)
    v = jnp.var(x, axis=axis, keepdims=True)
    return (x - m) / jnp.sqrt(v + eps)

def _scatter_add(tgt, idx, src, axis=0):
    return tgt.at[idx].add(src)

def _segment_sum(src, seg, n):
    return jax.ops.segment_sum(src, seg, n)
kernel_name = 'mk_seq_preln_d2_jaxref_r8_ca2968'

def setup_inputs(seed: int=0):
    np.random.seed(seed)
    _w = jnp.asarray

    def _L0_attn_setup():
        import jax, jax.numpy as jnp
        import numpy as np
        D_MODEL = 128
        D_INNER = 256
        D_STATE = 16
        D_CONV = 4
        DT_RANK = 128
        BATCH = 4
        SEQ = 256

        def silu(x):
            return x * jax.nn.sigmoid(x)

        def causal_depthwise_conv(x, w, b):
            lhs = jnp.moveaxis(x, 1, 2)
            rhs = w[:, None, :]
            y = jax.lax.conv_general_dilated(lhs, rhs, window_strides=(1,), padding=[(D_CONV - 1, 0)], dimension_numbers=('NCH', 'OIH', 'NCH'), feature_group_count=x.shape[-1])
            return jnp.moveaxis(y, 2, 1) + b

        def selective_scan(delta, Bm, Cm, u, A):
            dT = jnp.moveaxis(delta, 1, 0)
            BT = jnp.moveaxis(Bm, 1, 0)
            CT = jnp.moveaxis(Cm, 1, 0)
            uT = jnp.moveaxis(u, 1, 0)
            h0 = jnp.zeros((delta.shape[0], delta.shape[2], A.shape[1]), delta.dtype)

            def step(h, ins):
                d_t, B_t, C_t, u_t = ins
                h = jnp.exp(d_t[..., None] * A) * h + (d_t * u_t)[..., None] * B_t[:, None, :]
                y = jnp.einsum('bdn,bn->bd', h, C_t)
                return (h, y)
            _, yT = jax.lax.scan(step, h0, (dT, BT, CT, uT))
            return jnp.moveaxis(yT, 0, 1)
        key = jax.random.key(seed)
        ks = jax.random.split(key, 10)
        s = 0.02
        return {'x': jax.random.normal(ks[0], (BATCH, SEQ, D_MODEL), jnp.float32), 'W_in_o': jax.random.normal(ks[1], (D_MODEL, 2 * D_INNER), jnp.float32) * s, 'b_in_o': jnp.zeros((2 * D_INNER,), jnp.float32), 'W_out_o': jax.random.normal(ks[2], (D_INNER, D_MODEL), jnp.float32) * s, 'b_out_o': jnp.zeros((D_MODEL,), jnp.float32), 'W_in_i': jax.random.normal(ks[3], (D_INNER, 2 * D_INNER), jnp.float32) * s, 'conv_w': jax.random.normal(ks[4], (D_INNER, D_CONV), jnp.float32) * s, 'conv_b': jnp.zeros((D_INNER,), jnp.float32), 'W_xp': jax.random.normal(ks[5], (D_INNER, DT_RANK + 2 * D_STATE), jnp.float32) * s, 'W_dt': jax.random.normal(ks[6], (DT_RANK, D_INNER), jnp.float32) * s, 'b_dt': jnp.log(jnp.expm1(jax.random.uniform(ks[7], (D_INNER,), jnp.float32, 0.001, 0.1))), 'A_log': jnp.log(jnp.broadcast_to(jnp.arange(1, D_STATE + 1, dtype=jnp.float32), (D_INNER, D_STATE))), 'D_skip': jnp.ones((D_INNER,), jnp.float32), 'W_out_i': jax.random.normal(ks[8], (D_INNER, D_INNER), jnp.float32) * s}
    _L0_attn_in = _L0_attn_setup()

    def _L0_ffn_setup():
        import math
        import jax, jax.numpy as jnp
        import numpy as np
        B, S, D, H, E, F = (2, 128, 128, 16, 16, 512)
        HEAD = D // H
        MOE_TOKEN_DROPOUT = 0.2
        EPS = 1e-05

        def layer_norm(x, w, b):
            mu = x.mean(-1, keepdims=True)
            var = ((x - mu) ** 2).mean(-1, keepdims=True)
            return (x - mu) * jax.lax.rsqrt(var + EPS) * w + b
        key = jax.random.key(seed)
        ks = jax.random.split(key, 16)
        w = lambda k, shape: jax.random.normal(k, shape, jnp.float32) * 0.02
        return {'hidden_states': jax.random.normal(ks[0], (B, S, D), jnp.float32), 'ln1_w': jnp.ones((D,), jnp.float32), 'ln1_b': jnp.zeros((D,), jnp.float32), 'q_w': w(ks[1], (D, D)), 'q_b': jnp.zeros((D,), jnp.float32), 'k_w': w(ks[2], (D, D)), 'k_b': jnp.zeros((D,), jnp.float32), 'v_w': w(ks[3], (D, D)), 'v_b': jnp.zeros((D,), jnp.float32), 'o_w': w(ks[4], (D, D)), 'o_b': jnp.zeros((D,), jnp.float32), 'ln2_w': jnp.ones((D,), jnp.float32), 'ln2_b': jnp.zeros((D,), jnp.float32), 'router_w': w(ks[5], (D, E)), 'fc1_w': w(ks[6], (E, D, F)), 'fc1_b': jnp.zeros((E, F), jnp.float32), 'fc2_w': w(ks[7], (E, F, D)), 'fc2_b': jnp.zeros((E, D), jnp.float32)}
    _L0_ffn_in = _L0_ffn_setup()

    def _L1_attn_setup():
        import jax, jax.numpy as jnp
        import numpy as np
        from math import sqrt
        EMBED_DIM = 128
        NUM_HEADS = 16
        HEAD_DIM = EMBED_DIM // NUM_HEADS
        CAUSAL = True
        key = jax.random.key(seed)
        ks = jax.random.split(key, 5)
        B, S, E = (2, 256, EMBED_DIM)
        x = jax.random.normal(ks[0], (B, S, E), dtype=jnp.float32)
        scale = 1.0 / sqrt(E)
        Wq = jax.random.normal(ks[1], (E, E), dtype=jnp.float32) * scale
        Wk = jax.random.normal(ks[2], (E, E), dtype=jnp.float32) * scale
        Wv = jax.random.normal(ks[3], (E, E), dtype=jnp.float32) * scale
        Wo = jax.random.normal(ks[4], (E, E), dtype=jnp.float32) * scale
        return {'x': x, 'Wq': Wq, 'Wk': Wk, 'Wv': Wv, 'Wo': Wo}
    _L1_attn_in = _L1_attn_setup()

    def _L1_ffn_setup():
        import jax, jax.numpy as jnp
        import numpy as np
        D, H, E, K, S = (128, 256, 8, 2, 1)
        B, L = (4, 256)
        key = jax.random.key(seed)
        ks = jax.random.split(key, 9)
        std = 0.02
        return {'x': jax.random.normal(ks[0], (B, L, D), dtype=jnp.float32), 'router_w': jax.random.normal(ks[1], (E, D), dtype=jnp.float32) * std, 'experts_bias': jnp.zeros((E,), dtype=jnp.float32), 'w1': jax.random.normal(ks[2], (E, D, H), dtype=jnp.float32) * std, 'w3': jax.random.normal(ks[3], (E, D, H), dtype=jnp.float32) * std, 'w2': jax.random.normal(ks[4], (E, H, D), dtype=jnp.float32) * std, 'sw1': jax.random.normal(ks[5], (S, D, H), dtype=jnp.float32) * std, 'sw3': jax.random.normal(ks[6], (S, D, H), dtype=jnp.float32) * std, 'sw2': jax.random.normal(ks[7], (S, H, D), dtype=jnp.float32) * std}
    _L1_ffn_in = _L1_ffn_setup()
    _d = {'L0_attn_x': _L0_attn_in['x'], 'L0_attn_W_in_o': _L0_attn_in['W_in_o'], 'L0_attn_b_in_o': _L0_attn_in['b_in_o'], 'L0_attn_W_out_o': _L0_attn_in['W_out_o'], 'L0_attn_b_out_o': _L0_attn_in['b_out_o'], 'L0_attn_W_in_i': _L0_attn_in['W_in_i'], 'L0_attn_conv_w': _L0_attn_in['conv_w'], 'L0_attn_conv_b': _L0_attn_in['conv_b'], 'L0_attn_W_xp': _L0_attn_in['W_xp'], 'L0_attn_W_dt': _L0_attn_in['W_dt'], 'L0_attn_b_dt': _L0_attn_in['b_dt'], 'L0_attn_A_log': _L0_attn_in['A_log'], 'L0_attn_D_skip': _L0_attn_in['D_skip'], 'L0_attn_W_out_i': _L0_attn_in['W_out_i'], 'L0_ffn_ln1_w': _L0_ffn_in['ln1_w'], 'L0_ffn_ln1_b': _L0_ffn_in['ln1_b'], 'L0_ffn_q_w': _L0_ffn_in['q_w'], 'L0_ffn_q_b': _L0_ffn_in['q_b'], 'L0_ffn_k_w': _L0_ffn_in['k_w'], 'L0_ffn_k_b': _L0_ffn_in['k_b'], 'L0_ffn_v_w': _L0_ffn_in['v_w'], 'L0_ffn_v_b': _L0_ffn_in['v_b'], 'L0_ffn_o_w': _L0_ffn_in['o_w'], 'L0_ffn_o_b': _L0_ffn_in['o_b'], 'L0_ffn_ln2_w': _L0_ffn_in['ln2_w'], 'L0_ffn_ln2_b': _L0_ffn_in['ln2_b'], 'L0_ffn_router_w': _L0_ffn_in['router_w'], 'L0_ffn_fc1_w': _L0_ffn_in['fc1_w'], 'L0_ffn_fc1_b': _L0_ffn_in['fc1_b'], 'L0_ffn_fc2_w': _L0_ffn_in['fc2_w'], 'L0_ffn_fc2_b': _L0_ffn_in['fc2_b'], 'L1_attn_Wq': _L1_attn_in['Wq'], 'L1_attn_Wk': _L1_attn_in['Wk'], 'L1_attn_Wv': _L1_attn_in['Wv'], 'L1_attn_Wo': _L1_attn_in['Wo'], 'L1_ffn_router_w': _L1_ffn_in['router_w'], 'L1_ffn_experts_bias': _L1_ffn_in['experts_bias'], 'L1_ffn_w1': _L1_ffn_in['w1'], 'L1_ffn_w3': _L1_ffn_in['w3'], 'L1_ffn_w2': _L1_ffn_in['w2'], 'L1_ffn_sw1': _L1_ffn_in['sw1'], 'L1_ffn_sw3': _L1_ffn_in['sw3'], 'L1_ffn_sw2': _L1_ffn_in['sw2']}
    _x0 = _d['L0_attn_x']
    _d['L0_attn_x'] = jax.random.normal(jax.random.fold_in(jax.random.key(seed), 1), (1, 2048, 128), dtype=_x0.dtype)
    del _x0
    return _d

def reference(L0_attn_x, L0_attn_W_in_o, L0_attn_b_in_o, L0_attn_W_out_o, L0_attn_b_out_o, L0_attn_W_in_i, L0_attn_conv_w, L0_attn_conv_b, L0_attn_W_xp, L0_attn_W_dt, L0_attn_b_dt, L0_attn_A_log, L0_attn_D_skip, L0_attn_W_out_i, L0_ffn_ln1_w, L0_ffn_ln1_b, L0_ffn_q_w, L0_ffn_q_b, L0_ffn_k_w, L0_ffn_k_b, L0_ffn_v_w, L0_ffn_v_b, L0_ffn_o_w, L0_ffn_o_b, L0_ffn_ln2_w, L0_ffn_ln2_b, L0_ffn_router_w, L0_ffn_fc1_w, L0_ffn_fc1_b, L0_ffn_fc2_w, L0_ffn_fc2_b, L1_attn_Wq, L1_attn_Wk, L1_attn_Wv, L1_attn_Wo, L1_ffn_router_w, L1_ffn_experts_bias, L1_ffn_w1, L1_ffn_w3, L1_ffn_w2, L1_ffn_sw1, L1_ffn_sw3, L1_ffn_sw2):

    def _L0_attn_ref(x, W_in_o, b_in_o, W_out_o, b_out_o, W_in_i, conv_w, conv_b, W_xp, W_dt, b_dt, A_log, D_skip, W_out_i):
        import jax, jax.numpy as jnp
        import numpy as np
        D_MODEL = 128
        D_INNER = 256
        D_STATE = 16
        D_CONV = 4
        DT_RANK = 128
        BATCH = 4
        SEQ = 256

        def silu(x):
            return x * jax.nn.sigmoid(x)

        def causal_depthwise_conv(x, w, b):
            lhs = jnp.moveaxis(x, 1, 2)
            rhs = w[:, None, :]
            y = jax.lax.conv_general_dilated(lhs, rhs, window_strides=(1,), padding=[(D_CONV - 1, 0)], dimension_numbers=('NCH', 'OIH', 'NCH'), feature_group_count=x.shape[-1])
            return jnp.moveaxis(y, 2, 1) + b

        def selective_scan(delta, Bm, Cm, u, A):
            dT = jnp.moveaxis(delta, 1, 0)
            BT = jnp.moveaxis(Bm, 1, 0)
            CT = jnp.moveaxis(Cm, 1, 0)
            uT = jnp.moveaxis(u, 1, 0)
            h0 = jnp.zeros((delta.shape[0], delta.shape[2], A.shape[1]), delta.dtype)

            def step(h, ins):
                d_t, B_t, C_t, u_t = ins
                h = jnp.exp(d_t[..., None] * A) * h + (d_t * u_t)[..., None] * B_t[:, None, :]
                y = jnp.einsum('bdn,bn->bd', h, C_t)
                return (h, y)
            _, yT = jax.lax.scan(step, h0, (dT, BT, CT, uT))
            return jnp.moveaxis(yT, 0, 1)
        xz = x @ W_in_o + b_in_o
        x_proj, z_proj = (xz[..., :D_INNER], xz[..., D_INNER:])
        xz2 = x_proj @ W_in_i
        xm, zm = (xz2[..., :D_INNER], xz2[..., D_INNER:])
        xc = silu(causal_depthwise_conv(xm, conv_w, conv_b))
        dbl = xc @ W_xp
        dt = dbl[..., :DT_RANK]
        Bm = dbl[..., DT_RANK:DT_RANK + D_STATE]
        Cm = dbl[..., DT_RANK + D_STATE:]
        delta = jax.nn.softplus(dt @ W_dt + b_dt)
        A = -jnp.exp(A_log)
        y = selective_scan(delta, Bm, Cm, xc, A) + D_skip * xc
        y = y * silu(zm)
        out_i = y @ W_out_i
        out = out_i * jax.nn.sigmoid(z_proj)
        return out @ W_out_o + b_out_o

    def _L0_ffn_ref(hidden_states, ln1_w, ln1_b, q_w, q_b, k_w, k_b, v_w, v_b, o_w, o_b, ln2_w, ln2_b, router_w, fc1_w, fc1_b, fc2_w, fc2_b):
        import math
        import jax, jax.numpy as jnp
        import numpy as np
        B, S, D, H, E, F = (2, 128, 128, 16, 16, 512)
        HEAD = D // H
        MOE_TOKEN_DROPOUT = 0.2
        EPS = 1e-05

        def layer_norm(x, w, b):
            mu = x.mean(-1, keepdims=True)
            var = ((x - mu) ** 2).mean(-1, keepdims=True)
            return (x - mu) * jax.lax.rsqrt(var + EPS) * w + b
        b, s, _ = hidden_states.shape
        T = b * s
        neg = jnp.finfo(jnp.float32).min
        resid = hidden_states
        x = layer_norm(hidden_states, ln1_w, ln1_b)
        q = (x @ q_w + q_b) / math.sqrt(HEAD)
        k = x @ k_w + k_b
        v = x @ v_w + v_b
        split = lambda t: t.reshape(b, s, H, HEAD).transpose(0, 2, 1, 3)
        q, k, v = (split(q), split(k), split(v))
        scores = jnp.einsum('bhqd,bhkd->bhqk', q, k)
        causal = jnp.tril(jnp.ones((s, s), bool))
        scores = jnp.where(causal, scores, neg)
        attn = jax.nn.softmax(scores, axis=-1)
        ctx = jnp.einsum('bhqk,bhkd->bhqd', attn, v)
        ctx = ctx.transpose(0, 2, 1, 3).reshape(b, s, D)
        hidden = resid + (ctx @ o_w + o_b)
        resid = hidden
        xt = layer_norm(hidden, ln2_w, ln2_b).reshape(T, D)
        logits = xt @ router_w
        probs = jax.nn.softmax(logits, axis=-1)
        top1 = jnp.argmax(probs, axis=-1)
        m1 = jax.nn.one_hot(top1, E, dtype=jnp.float32)
        logits_no1 = jnp.where(m1 > 0, -jnp.inf, logits)
        top2 = jnp.argmax(logits_no1, axis=-1)
        m2 = jax.nn.one_hot(top2, E, dtype=jnp.float32)
        loc1 = jnp.cumsum(m1, axis=0) - 1.0
        loc2 = jnp.cumsum(m2, axis=0) - 1.0 + m1.sum(axis=0, keepdims=True)
        C = 2 * math.ceil(T / E)
        m1 = m1 * (loc1 < C)
        m2 = m2 * (loc2 < C)
        g1 = (probs * m1).sum(-1)
        g2 = (probs * m2).sum(-1)
        denom = jnp.maximum(g1 + g2, jnp.finfo(jnp.float32).eps)
        g1, g2 = (g1 / denom, g2 / denom)
        slot1 = (loc1 * m1).sum(-1).astype(jnp.int32)
        slot2 = (loc2 * m2).sum(-1).astype(jnp.int32)
        d1 = m1[:, :, None] * jax.nn.one_hot(slot1, C, dtype=jnp.float32)[:, None, :]
        d2 = m2[:, :, None] * jax.nn.one_hot(slot2, C, dtype=jnp.float32)[:, None, :]
        dispatch = d1 + d2
        combine = g1[:, None, None] * d1 + g2[:, None, None] * d2
        xin = jnp.einsum('tec,td->ecd', dispatch, xt)
        h = jnp.einsum('ecd,edf->ecf', xin, fc1_w) + fc1_b[:, None, :]
        h = jax.nn.gelu(h, approximate=False)
        eout = jnp.einsum('ecf,efd->ecd', h, fc2_w) + fc2_b[:, None, :]
        eout = eout * (1.0 - MOE_TOKEN_DROPOUT)
        moe_out = jnp.einsum('tec,ecd->td', combine, eout).reshape(b, s, D)
        return resid + moe_out

    def _L1_attn_ref(x, Wq, Wk, Wv, Wo):
        import jax, jax.numpy as jnp
        import numpy as np
        from math import sqrt
        EMBED_DIM = 128
        NUM_HEADS = 16
        HEAD_DIM = EMBED_DIM // NUM_HEADS
        CAUSAL = True
        B, S, E = x.shape
        H, D = (NUM_HEADS, HEAD_DIM)

        def proj(W):
            y = jnp.einsum('bse,fe->bsf', x, W)
            return y.reshape(B, S, H, D).transpose(0, 2, 1, 3)
        q, k, v = (proj(Wq), proj(Wk), proj(Wv))
        scores = jnp.einsum('bhsd,bhtd->bhst', q, k)
        if CAUSAL:
            mask = jnp.triu(jnp.ones((S, S), dtype=bool), k=1)
            scores = jnp.where(mask, -jnp.inf, scores)
        attn = jax.nn.softmax(scores / sqrt(D), axis=-1)
        out = jnp.einsum('bhst,bhtd->bhsd', attn, v)
        out = out.transpose(0, 2, 1, 3).reshape(B, S, E)
        return jnp.einsum('bse,fe->bsf', out, Wo)

    def _L1_ffn_ref(x, router_w, experts_bias, w1, w3, w2, sw1, sw3, sw2):
        import jax, jax.numpy as jnp
        import numpy as np
        D, H, E, K, S = (128, 256, 8, 2, 1)
        B, L = (4, 256)
        b, l, d = x.shape
        xf = x.reshape(-1, d)
        sg = jnp.einsum('td,sdh->tsh', xf, sw1)
        su = jnp.einsum('td,sdh->tsh', xf, sw3)
        shared_out = jnp.einsum('tsh,shd->td', jax.nn.silu(sg) * su, sw2)
        logits = xf @ router_w.T + experts_bias
        rw, sel = jax.lax.top_k(logits, K)
        rw = jax.nn.softmax(rw.astype(jnp.float32), axis=-1).astype(x.dtype)
        cw = (jax.nn.one_hot(sel, E, dtype=x.dtype) * rw[..., None]).sum(axis=1)
        g = jnp.einsum('td,edh->teh', xf, w1)
        u = jnp.einsum('td,edh->teh', xf, w3)
        eo = jax.nn.silu(g) * u
        moe_out = jnp.einsum('te,teh,ehd->td', cw, eo, w2)
        return (moe_out + shared_out).reshape(b, l, d)
    x = L0_attn_x
    x = x + _L0_attn_ref(_layernorm(x, axis=-1), L0_attn_W_in_o, L0_attn_b_in_o, L0_attn_W_out_o, L0_attn_b_out_o, L0_attn_W_in_i, L0_attn_conv_w, L0_attn_conv_b, L0_attn_W_xp, L0_attn_W_dt, L0_attn_b_dt, L0_attn_A_log, L0_attn_D_skip, L0_attn_W_out_i)
    x = x + _L0_ffn_ref(_layernorm(x, axis=-1), L0_ffn_ln1_w, L0_ffn_ln1_b, L0_ffn_q_w, L0_ffn_q_b, L0_ffn_k_w, L0_ffn_k_b, L0_ffn_v_w, L0_ffn_v_b, L0_ffn_o_w, L0_ffn_o_b, L0_ffn_ln2_w, L0_ffn_ln2_b, L0_ffn_router_w, L0_ffn_fc1_w, L0_ffn_fc1_b, L0_ffn_fc2_w, L0_ffn_fc2_b)
    x = x + _L1_attn_ref(_layernorm(x, axis=-1), L1_attn_Wq, L1_attn_Wk, L1_attn_Wv, L1_attn_Wo)
    x = x + _L1_ffn_ref(_layernorm(x, axis=-1), L1_ffn_router_w, L1_ffn_experts_bias, L1_ffn_w1, L1_ffn_w3, L1_ffn_w2, L1_ffn_sw1, L1_ffn_sw3, L1_ffn_sw2)
    return x

_drawn_inputs = setup_inputs


def setup_inputs(seed=0):
    import zlib

    import numpy as np

    out = dict(_drawn_inputs(seed))
    spreads = {'L0_attn_b_in_o': (0.0, 0.8),
     'L0_attn_b_out_o': (0.0, 0.8),
     'L0_attn_conv_b': (0.0, 0.8),
     'L0_attn_D_skip': (1.0, 0.6),
     'L0_ffn_ln1_w': (1.0, 0.6),
     'L0_ffn_ln1_b': (0.0, 0.8),
     'L0_ffn_q_b': (0.0, 0.8),
     'L0_ffn_k_b': (0.0, 2.0),
     'L0_ffn_v_b': (0.0, 1.697),
     'L0_ffn_o_b': (0.0, 0.8),
     'L0_ffn_ln2_w': (1.0, 0.6),
     'L0_ffn_ln2_b': (0.0, 1.676),
     'L0_ffn_fc1_b': (0.0, 2.0),
     'L0_ffn_fc2_b': (0.0, 0.8),
     'L1_ffn_experts_bias': (0.0, 0.8)}
    factors = {'L0_attn_W_in_o': 8.0,
     'L0_attn_W_out_o': 8.0,
     'L0_attn_W_in_i': 8.0,
     'L0_attn_conv_w': 8.0,
     'L0_attn_W_xp': 8.0,
     'L0_attn_W_dt': 8.0,
     'L0_attn_b_dt': 8.0,
     'L0_attn_A_log': 8.0,
     'L0_attn_W_out_i': 8.0,
     'L0_ffn_q_w': 8.0,
     'L0_ffn_k_w': 8.0,
     'L0_ffn_v_w': 7.356,
     'L0_ffn_o_w': 3.924,
     'L0_ffn_fc1_w': 3.216,
     'L0_ffn_fc2_w': 2.914,
     'L1_ffn_router_w': 8.0,
     'L1_ffn_w1': 8.0,
     'L1_ffn_w3': 8.0,
     'L1_ffn_w2': 8.0,
     'L1_ffn_sw1': 8.0,
     'L1_ffn_sw3': 8.0,
     'L1_ffn_sw2': 8.0,
     'L1_attn_Wq': 6.724,
     'L1_attn_Wk': 7.357,
     'L1_attn_Wv': 3.53,
     'L1_attn_Wo': 3.807}
    for name, (base, spread) in spreads.items():
        noise = np.random.default_rng([zlib.crc32(name.encode()), seed]).standard_normal(out[name].shape)
        drawn = base * np.exp(spread * noise) if base else spread * noise
        out[name] = jnp.asarray(drawn.astype(out[name].dtype))
    for name, factor in factors.items():
        out[name] = (out[name] * factor).astype(out[name].dtype)
    return out
```

```python
from contextlib import ExitStack

import concourse.bass as bass
from concourse import mybir

ALU = mybir.AluOpType
ACT = mybir.ActivationFunctionType
AX = mybir.AxisListType
F32 = mybir.dt.float32
BF16 = mybir.dt.bfloat16
I32 = mybir.dt.int32

P = 128
T = 2048
D = 128
NT = T // P
CW = 512
NC = T // CW
DI = 256
NM = DI // P
NS = 16
HALF = T // 2
EPS = 1e-5
NEG = -3.0e38
NH = 16
HD = D // NH
SCORE_SCALE = HD ** -0.5
ROWS = 9 * HD
E0, F0, CAP = 16, 512, 2 * (T // 16)
E1, F1 = 8, 256
SLOTS = E0 * CAP


def ds(i, n):
    return bass.ds(i * n, n)


def program(nc, a, out):
    with ExitStack() as ctx:
        ctx.enter_context(nc.allow_non_contiguous_dma(reason="small per-channel vectors"))

        def sb(name, shape, dt=F32):
            return ctx.enter_context(nc.sbuf_tensor(name, shape, dt))

        def sem(name):
            return ctx.enter_context(nc.semaphore(name))

        arena = sb("arena", [P, 18, T])
        extra = sb("extra", [P, 4112])
        psum_a = ctx.enter_context(nc.psum_tensor("psum_a", [P, T], F32))
        psum_b = ctx.enter_context(nc.psum_tensor("psum_b", [P, T], F32))
        psum_ab = [psum_a, psum_b]

        def slot(i):
            return arena[:, i, :]

        def pair(i):
            return arena[:, i:i + 2, :]

        def tiled(ap):
            return ap.rearrange("p (t d) -> p t d", d=D)

        ident = sb("ident", [P, P])
        ident_bf = sb("ident_bf", [P, P], BF16)
        ones_row = sb("ones_row", [1, P])
        ones_bf = sb("ones_bf", [P, P], BF16)
        tri_bf = sb("tri_bf", [P, P], BF16)
        mask_q = sb("mask_q", [P, P], BF16)
        mask_k = sb("mask_k", [P, CW], BF16)
        select = sb("select", [96, 2 * NS, P], BF16)
        sum_groups = sb("sum_groups", [P, HD + 1])
        w_in_o = sb("w_in_o", [P, 2 * DI])
        w_in_i = sb("w_in_i", [P, NM, 2 * DI])
        w_xp = sb("w_xp", [P, NM, P + 2 * NS])
        w_dt = sb("w_dt", [P, DI])
        w_out_i = sb("w_out_i", [P, NM, DI])
        w_out_o = sb("w_out_o", [P, NM, D])
        vec = sb("vec", [P, 64])
        b_in, conv_b, b_dt, d_skip = vec[:, 0:4], vec[:, 4:6], vec[:, 6:8], vec[:, 8:10]
        conv_w = vec[:, 16:24].rearrange("p (m k) -> p m k", m=NM)
        q_b, k_b = vec[:, 24:25], vec[:, 25:26]
        a_neg = sb("a_neg", [P, NM, NS])
        rows = sb("rows", [P, 7, D])
        b_out_row, ln1_w, ln1_b, v_b_row, o_b_row, ln2_w, ln2_b = (rows[:, i, :] for i in range(7))
        w_att = [sb(f"w_att{i}", [P, 4, D]) for i in range(2)]
        w_raw = sb("w_raw", [P, 4, D])
        stats = sb("stats", [P, NT, 6])
        meanvar = sb("meanvar", [P, NT, 2])
        spread = sb("spread", [P, NT])
        carry = sb("carry", [P, NM, NS])

        x_loaded = sem("x_loaded")
        mamba_weights_loaded = sem("mamba_weights_loaded")
        attention_weights_loaded = sem("attention_weights_loaded")
        consts_zeroed = sem("consts_zeroed")
        consts_ready = sem("consts_ready")
        NCONST = 9
        dve_step = sem("dve_step")
        act_step = sem("act_step")
        pool_step = sem("pool_step")
        NORMS = ["ln_a", "ln_b", "ln_b1", "ln_b2", "ln_c", "ln_d"]
        tile_stats, tile_aggr, var_ready, std_ready, rstd_ready, tile_normed = (
            sem(n) for n in ("tile_stats", "tile_aggr", "var_ready", "std_ready", "rstd_ready", "tile_normed"))

        def normed(name):
            return NT * (NORMS.index(name) + 1)

        counts = {"dve": 0, "act": 0, "pool": 0}

        def dve_link(e, ins):
            counts["dve"] += 1
            ins.then_inc(dve_step, 1)
            e.wait_ge(dve_step, counts["dve"])

        def act_link(e, ins):
            counts["act"] += 1
            ins.then_inc(act_step, 1)
            e.wait_ge(act_step, counts["act"])

        def pool_link(e, ins):
            counts["pool"] += 1
            ins.then_inc(pool_step, 1)
            e.wait_ge(pool_step, counts["pool"])

        def norm_dve(e, name, src, dst):
            n = NORMS.index(name)
            with e.Fori(0, NT) as t:
                e.bn_stats(stats[:, bass.ds(t, 1), :].rearrange("p a b -> p (a b)"), src[:, ds(t, D)]).then_inc(tile_stats, 1)
            e.wait_ge(tile_stats, NT * (n + 1))
            for t in range(NT):
                e.bn_aggr(meanvar[:, t, :], stats[:, t, :]).then_inc(tile_aggr, 1)
            e.wait_ge(tile_aggr, NT * (n + 1))
            e.tensor_scalar(spread[:, :], meanvar[:, :, 1], EPS, None, ALU.add).then_inc(var_ready, 1)
            e.wait_ge(std_ready, n + 1)
            e.reciprocal(spread[:, :], spread[:, :]).then_inc(rstd_ready, 1)
            e.wait_ge(rstd_ready, n + 1)
            with e.Fori(0, NT) as t:
                e.tensor_scalar(dst[:, ds(t, D)], src[:, ds(t, D)], meanvar[:, bass.ds(t, 1), 0],
                                spread[:, bass.ds(t, 1)], ALU.subtract, ALU.mult).then_inc(tile_normed, 1)
            e.wait_ge(tile_normed, normed(name))

        def norm_act(e, name):
            e.wait_ge(var_ready, NORMS.index(name) + 1)
            e.activation(spread[:, :], spread[:, :], ACT.Sqrt).then_inc(std_ready, 1)

        x_tok = slot(0)
        xn, xT = slot(1), slot(2)
        x_proj = [slot(3), slot(4)]
        gate_out = [slot(5), slot(6)]
        xm = extra[:, 0:2 * 2056].rearrange("p (m n) -> p m n", m=NM)
        conv = [slot(7), slot(8)]
        xc = pair(9)
        gate_in = pair(11)
        dtT = slot(3)
        bc32 = arena[0:32, 4, :]
        bc_parts = arena[0:96, 16, :].bitcast(BF16)[:, 0:T]
        delta = pair(7)
        sp_z, sp_w, sp_l = slot(13), slot(14), slot(15)
        du = pair(13)
        dA = [arena[:, 2 + b, :].rearrange("p (m n) -> p m n", m=NM) for b in range(2)]
        dBu = [arena[:, i, :].rearrange("p (m n) -> p m n", m=NM) for i in (4, 1)]
        c_copy = extra[:, 0:HALF]
        hs = arena[:, 15, :].rearrange("p (m n) -> p m n", m=NM)
        hc = arena[:, 17, :].rearrange("p (m n) -> p m n", m=NM)
        out_i = pair(7)
        x1 = slot(1)

        piece_filled = sem("piece_filled")
        piece_freed = sem("piece_freed")
        x_scaled = sem("x_with_bias")
        xm_padded = sem("xm_padded")
        conv_done = sem("conv_done")
        xc_ready = sem("xc_ready")
        bc_split = sem("bc_split")
        sp_z_ready, sp_w_ready, sp_l_ready, delta_ready = (sem(n) for n in ("sp_z_ready", "sp_w_ready", "sp_l_ready", "delta_ready"))
        du_ready = sem("du_ready")
        a_exp = sem("a_exp")
        a_ready = sem("a_ready")
        b_spread, c_spread = sem("b_spread"), sem("c_spread")
        dA_ready = sem("dA_ready")
        dBu_done = sem("dBu_done")
        scan_done = sem("scan_done")
        hc0_done, hc1_done = sem("hc0_done"), sem("hc1_done")
        c_copied = sem("c_copied")
        y_added = sem("y_added")
        yg_ready = sem("yg_ready")
        x1_ready = sem("x1_ready")

        def mamba_loads(e):
            e.dma_start(tiled(x_tok), a["L0_attn_x"].rearrange("b (t p) d -> p (b t) d", p=P)).then_inc(x_loaded, 16)
            loads = [
                (w_in_o[:, :], a["L0_attn_W_in_o"]),
                (b_in, a["L0_attn_b_in_o"].rearrange("(m p) -> p m", p=P)),
                (w_in_i[:, :, :], a["L0_attn_W_in_i"].rearrange("(k p) n -> p k n", p=P)),
                (conv_w, a["L0_attn_conv_w"].rearrange("(m p) k -> p m k", p=P)),
                (conv_b, a["L0_attn_conv_b"].rearrange("(m p) -> p m", p=P)),
                (w_xp[:, :, :], a["L0_attn_W_xp"].rearrange("(k p) n -> p k n", p=P)),
                (w_dt[:, :], a["L0_attn_W_dt"]),
                (b_dt, a["L0_attn_b_dt"].rearrange("(m p) -> p m", p=P)),
                (a_neg[:, :, :], a["L0_attn_A_log"].rearrange("(m p) n -> p m n", p=P)),
                (d_skip, a["L0_attn_D_skip"].rearrange("(m p) -> p m", p=P)),
                (w_out_i[:, :, :], a["L0_attn_W_out_i"].rearrange("(k p) n -> p k n", p=P)),
                (w_out_o[:, :, :], a["L0_attn_W_out_o"].rearrange("(k p) n -> p k n", p=P)),
                (b_out_row, row_of(a["L0_attn_b_out_o"])),
            ]
            for dst, src in loads:
                e.dma_start(dst, src).then_inc(mamba_weights_loaded, 16)
        MAMBA_LOADS = 13

        def row_of(v):
            return v.rearrange("(a n) -> a n", a=1).to_broadcast([P, v.shape[0]])

        def constants_pool(e):
            for i, (m, v) in enumerate([(ident[:, :], 0.0), (ident_bf[:, :], 0.0), (mask_q[:, :], 0.0),
                                        (tri_bf[:, :], 1.0), (mask_k[:, :], 0.0), (select[:, :, :], 0.0),
                                        (sum_groups[:, :], 0.0), (ones_bf[:, :], 1.0), (ones_row[:, :], 1.0)]):
                e.memset(m, v).then_inc(consts_zeroed, 1)
            e.wait_ge(consts_zeroed, 9)
            for m in (ident, ident_bf):
                e.affine_select(out=m[:, :], in_=m[:, :], compare_op=ALU.not_equal, fill=1.0, base=0,
                                pattern=[[-1, P]], channel_multiplier=1).then_inc(consts_ready, 1)
            e.affine_select(out=mask_q[:, :], in_=mask_q[:, :], compare_op=ALU.is_ge, fill=NEG, base=0,
                            pattern=[[-1, P]], channel_multiplier=1).then_inc(consts_ready, 1)
            e.affine_select(out=tri_bf[:, :], in_=tri_bf[:, :], compare_op=ALU.is_ge, fill=0.0, base=0,
                            pattern=[[1, P]], channel_multiplier=-1).then_inc(consts_ready, 1)
            e.affine_select(out=mask_k[:, :], in_=mask_k[:, :], compare_op=ALU.is_ge, fill=NEG, base=P - CW,
                            pattern=[[1, CW]], channel_multiplier=-1).then_inc(consts_ready, 1)
            for g in range(3):
                e.wait_ge(consts_ready, 5 + g)
                e.affine_select(out=select[32 * g:32 * g + 32, :, :], in_=select[32 * g:32 * g + 32, :, :],
                                compare_op=ALU.not_equal, fill=1.0, base=0,
                                pattern=[[-1, 2 * NS], [0, P]], channel_multiplier=1).then_inc(consts_ready, 1)
            for g in range(4):
                e.wait_ge(consts_ready, 8 + g)
                e.affine_select(out=sum_groups[32 * g:32 * g + 32, :], in_=sum_groups[32 * g:32 * g + 32, :],
                                compare_op=ALU.not_equal, fill=1.0, base=0,
                                pattern=[[-1, HD + 1]], channel_multiplier=1).then_inc(consts_ready, 1)
        CONSTS = 12

        def mamba_pool(e):
            e.wait_ge(consts_ready, CONSTS)
            e.memset(xm[:, :, 0:3], 0.0).then_inc(xm_padded, 1)
            e.wait_ge(mamba_weights_loaded, 16 * MAMBA_LOADS)
            e.wait_ge(tile_normed, normed("ln_a"))
            e.tensor_tensor(tiled(x_tok), tiled(x_tok), b_out_row.unsqueeze(1).to_broadcast([P, NT, D]), ALU.add).then_inc(x_scaled, 1)

            def state(step, first=False):
                e.wait_ge(c_copied, step + 1)
                e.wait_ge(scan_done, 2 * step + 1)
                if not first:
                    e.wait_ge(y_added, 2 * step - 1)
                e.tensor_tensor(hc[:, 0, :], hs[:, 0, :], c_copy, ALU.mult).then_inc(hc0_done, 1)
            state(0, first=True)
            with e.Fori(1, 2 * NS) as step:
                state(step)

        def mamba_pe(e):
            e.wait_ge(consts_ready, CONSTS)
            e.wait_ge(mamba_weights_loaded, 16 * MAMBA_LOADS)

            def piece(n, emit, free=None):
                if n >= 2:
                    e.wait_ge(piece_freed, n - 1)
                emit(psum_ab[n % 2]).then_inc(piece_filled, 1)

            def transposes(ps):
                for t in range(NT):
                    i = e.transpose(ps[:, t * P:(t + 1) * P], xn[:, t * P:(t + 1) * P], ident[:, :])
                return i

            def product(lhs, rhs, m=P):
                def emit(ps):
                    for c in range(NC):
                        for k in range(len(lhs)):
                            i = e.matmul(ps[0:m, c * CW:(c + 1) * CW], lhs[k], rhs[k][:, c * CW:(c + 1) * CW],
                                         start=(k == 0), stop=(k == len(lhs) - 1))
                    return i
                return emit

            e.wait_ge(tile_normed, normed("ln_a"))
            piece(0, transposes)
            e.wait_ge(piece_freed, 1)
            for m in range(4):
                piece(1 + m, product([w_in_o[:, m * P:(m + 1) * P]], [xT]))
            e.wait_ge(piece_freed, 3)
            for m in range(4):
                piece(5 + m, product([w_in_i[:, k, m * P:(m + 1) * P] for k in range(NM)], x_proj))
            e.wait_ge(xc_ready, NM)
            piece(9, product([w_xp[:, k, 0:P] for k in range(NM)], [xc[:, k, :] for k in range(NM)]))
            piece(10, product([w_xp[:, k, P:P + 2 * NS] for k in range(NM)], [xc[:, k, :] for k in range(NM)], 2 * NS))
            e.wait_ge(piece_freed, 10)
            for m in range(NM):
                piece(11 + m, product([w_dt[:, m * P:(m + 1) * P]], [dtT]))
            e.wait_ge(piece_freed, 13)
            e.wait_ge(bc_split, 1)

            for h in range(2):
                if h:
                    e.wait_ge(yg_ready, h)
                cols = slice(h * HALF, (h + 1) * HALF)

                def spread_row(r, dst, done):
                    for c in range(2):
                        i = e.matmul(dst[:, c * CW:(c + 1) * CW], select[:, bass.ds(r, 1), :].rearrange("p a b -> p (a b)"),
                                     bc_parts[:, h * HALF + c * CW:h * HALF + (c + 1) * CW], start=True, stop=True)
                    i.then_inc(done, 1)

                def add_y(m, step, start, stop):
                    e.wait_ge((hc0_done, hc1_done)[m], step + 1)
                    for c in range(2):
                        i = e.matmul(psum_b[:, m * HALF + c * CW:m * HALF + (c + 1) * CW], ident[:, :],
                                     hc[:, m, c * CW:(c + 1) * CW], start=start, stop=stop, skip_group_check=True)
                    i.then_inc(y_added, 1)

                if h:
                    e.wait_ge(dBu_done, NS * h)
                spread_row(0, psum_a[:, 0:HALF], b_spread)
                if h:
                    e.wait_ge(hc1_done, NS * h)
                    e.wait_ge(c_copied, NS * h)
                spread_row(NS, psum_a[:, HALF:T], c_spread)

                def state(n, first=False, ahead=True):
                    step = h * NS + n
                    e.wait_ge(hc1_done, step + 1)
                    e.wait_ge(c_copied, step + 1)
                    spread_row(NS + n + 1, psum_a[:, HALF:T], c_spread)
                    if ahead:
                        e.wait_ge(dBu_done, step + 2)
                        spread_row(n + 2, psum_a[:, 0:HALF], b_spread)
                    for m in range(NM):
                        add_y(m, step, first, False)

                e.wait_ge(dBu_done, h * NS + 1)
                spread_row(1, psum_a[:, 0:HALF], b_spread)
                state(0, first=True)
                with e.Fori(1, NS - 2) as n:
                    state(n)
                state(NS - 2, ahead=False)
                for m in range(NM):
                    add_y(m, h * NS + NS - 1, False, True)

            def out_tokens(ps):
                for t in range(NT):
                    for k in range(NM):
                        i = e.matmul(ps[:, t * P:(t + 1) * P], out_i[:, k, t * P:(t + 1) * P], w_out_o[:, k, :],
                                     start=(k == 0), stop=(k == NM - 1))
                return i

            e.wait_ge(yg_ready, 2)
            for m in range(NM):
                piece(13 + m, product([w_out_i[:, k, m * P:(m + 1) * P] for k in range(NM)], [gate_in[:, k, :] for k in range(NM)]))
            e.wait_ge(piece_freed, 15)
            piece(15, out_tokens)

        def mamba_act(e):
            e.wait_ge(mamba_weights_loaded, 16 * MAMBA_LOADS)
            norm_act(e, "ln_a")
            e.activation(a_neg[:, :, :], a_neg[:, :, :], ACT.Exp).then_inc(a_exp, 1)

            def read(n, dst, func, bias=None, m=P):
                e.wait_ge(piece_filled, n + 1)
                if bias is None:
                    e.activation(dst, psum_ab[n % 2][0:m, :], func).then_inc(piece_freed, 1)
                else:
                    e.activation(dst, psum_ab[n % 2][0:m, :], func, bias=bias).then_inc(piece_freed, 1)

            read(0, xT, ACT.Copy)
            for m in range(NM):
                read(1 + m, x_proj[m], ACT.Identity, b_in[:, m:m + 1])
            for m in range(NM):
                read(3 + m, gate_out[m], ACT.Sigmoid, b_in[:, 2 + m:3 + m])
            for m in range(NM):
                read(5 + m, xm[:, m, 3:3 + T], ACT.Copy)
            for m in range(NM):
                read(7 + m, gate_in[:, m, :], ACT.Silu)
            for m in range(NM):
                e.wait_ge(conv_done, m + 1)
                e.activation(xc[:, m, :], conv[m], ACT.Silu).then_inc(xc_ready, 1)
            read(9, dtT, ACT.Copy)
            read(10, bc32, ACT.Copy, m=32)
            for m in range(NM):
                read(11 + m, delta[:, m, :], ACT.Identity, b_dt[:, m:m + 1])
            e.wait_ge(piece_freed, 13)
            for m in range(NM):
                if m:
                    e.wait_ge(delta_ready, m)
                act_link(e, e.activation(sp_z, delta[:, m, :], ACT.Abs))
                e.activation(sp_z, sp_z, ACT.Exp, scale=-1.0).then_inc(sp_z_ready, 1)
                e.wait_ge(sp_w_ready, m + 1)
                e.activation(sp_l, sp_w, ACT.Ln).then_inc(sp_l_ready, 1)
            e.wait_ge(delta_ready, NM)
            e.wait_ge(a_ready, 1)

            def decay(h, n, b, first=False):
                if not first:
                    e.wait_ge(scan_done, 2 * (h * NS + n) - 2)
                for m in range(NM):
                    e.activation(dA[b][:, m, :], delta[:, m, h * HALF:(h + 1) * HALF], ACT.Exp,
                                 scale=a_neg[:, m, bass.ds(n, 1)]).then_inc(dA_ready, 1)
            def copy_c(step, first=False):
                e.wait_ge(c_spread, step + 1)
                if not first:
                    e.wait_ge(hc0_done, step)
                e.activation(c_copy, psum_a[:, HALF:T], ACT.Copy).then_inc(c_copied, 1)

            for h in range(2):
                decay(h, 0, 0, first=(h == 0))
                copy_c(h * NS, first=(h == 0))
                decay(h, 1, 1, first=(h == 0))
                with e.Fori(1, NS // 2) as i:
                    copy_c(h * NS + 2 * i - 1)
                    decay(h, 2 * i, 0)
                    copy_c(h * NS + 2 * i)
                    decay(h, 2 * i + 1, 1)
                copy_c(h * NS + NS - 1)

        def mamba_dve(e):
            e.wait_ge(x_loaded, 16)
            norm_dve(e, "ln_a", x_tok, xn)
            e.wait_ge(a_exp, 1)
            e.tensor_scalar(a_neg[:, :, :], a_neg[:, :, :], -1.0, None, ALU.mult).then_inc(a_ready, 1)
            e.wait_ge(xm_padded, 1)
            e.wait_ge(mamba_weights_loaded, 16 * MAMBA_LOADS)
            for m in range(NM):
                e.wait_ge(piece_freed, 6 + m)
                dve_link(e, e.tensor_scalar(conv[m], xm[:, m, 0:T], conv_w[:, m, 0:1], conv_b[:, m:m + 1], ALU.mult, ALU.add))
                for k in range(1, 4):
                    i = e.scalar_tensor_tensor(conv[m], xm[:, m, k:k + T], conv_w[:, m, k:k + 1], conv[m], ALU.mult, ALU.add)
                    if k < 3:
                        dve_link(e, i)
                    else:
                        i.then_inc(conv_done, 1)
            e.wait_ge(piece_freed, 11)
            rest = arena[0:32, 17, :]
            dve_link(e, e.tensor_copy(bc_parts[0:32, :], bc32))
            dve_link(e, e.tensor_tensor(rest, bc32, bc_parts[0:32, :], ALU.subtract))
            dve_link(e, e.tensor_copy(bc_parts[32:64, :], rest))
            dve_link(e, e.tensor_copy(arena[0:32, 16, 1024:2048].bitcast(BF16), rest))
            dve_link(e, e.tensor_tensor(rest, rest, arena[0:32, 16, 1024:2048].bitcast(BF16), ALU.subtract))
            e.tensor_copy(bc_parts[64:96, :], rest).then_inc(bc_split, 1)
            e.wait_ge(piece_freed, 13)
            for m in range(NM):
                e.wait_ge(sp_z_ready, m + 1)
                e.tensor_scalar(sp_w, sp_z, 1.0, None, ALU.add).then_inc(sp_w_ready, 1)
                e.wait_ge(sp_l_ready, m + 1)
                dve_link(e, e.scalar_tensor_tensor(sp_z, sp_w, -1.0, sp_z, ALU.add, ALU.subtract))
                dve_link(e, e.scalar_tensor_tensor(sp_l, delta[:, m, :], 0.0, sp_l, ALU.max, ALU.add))
                e.tensor_tensor(delta[:, m, :], sp_l, sp_z, ALU.subtract).then_inc(delta_ready, 1)
                e.wait_ge(delta_ready, m + 1)
            e.tensor_tensor(du, delta, xc, ALU.mult).then_inc(du_ready, 1)
            e.wait_ge(du_ready, 1)

            for h in range(2):
                cols = slice(h * HALF, (h + 1) * HALF)

                def weighted_input(n, b):
                    e.wait_ge(b_spread, h * NS + n + 1)
                    e.tensor_tensor(dBu[b], du[:, :, cols], psum_a[:, 0:HALF].unsqueeze(1).to_broadcast([P, NM, HALF]),
                                    ALU.mult).then_inc(dBu_done, 1)

                def state(n, b, first=False, last=False):
                    step = h * NS + n
                    e.wait_ge(dBu_done, step + 1)
                    if not first:
                        e.wait_ge(hc0_done, step)
                        e.wait_ge(hc1_done, step)
                    for m in range(NM):
                        e.wait_ge(dA_ready, 2 * step + m + 1)
                        start = 0.0 if h == 0 else carry[:, m, bass.ds(n, 1)]
                        e.tensor_tensor_scan(hs[:, m, :], dA[b][:, m, :], dBu[b][:, m, :], start, ALU.mult, ALU.add).then_inc(scan_done, 1)
                    if not last:
                        weighted_input(n + 1, 1 - b)
                    e.wait_ge(scan_done, 2 * step + 2)
                    if h == 0:
                        e.tensor_copy(carry[:, :, bass.ds(n, 1)], hs[:, :, HALF - 1:HALF])
                    e.wait_ge(c_copied, step + 1)
                    if not first:
                        e.wait_ge(y_added, 2 * step)
                    e.tensor_tensor(hc[:, 1, :], hs[:, 1, :], psum_a[:, HALF:T], ALU.mult).then_inc(hc1_done, 1)

                weighted_input(0, 0)
                state(0, 0, first=(h == 0))
                state(1, 1)
                with e.Fori(1, NS // 2 - 1) as i:
                    state(2 * i, 0)
                    state(2 * i + 1, 1)
                state(NS - 2, 0)
                state(NS - 1, 1, last=True)
                e.wait_ge(y_added, (h + 1) * 2 * NS)
                for m in range(NM):
                    i = e.scalar_tensor_tensor(hs[:, m, :], xc[:, m, cols], d_skip[:, m:m + 1],
                                               psum_b[:, m * HALF:(m + 1) * HALF], ALU.mult, ALU.add)
                    dve_link(e, i)
                e.tensor_tensor(gate_in[:, :, cols], hs, gate_in[:, :, cols], ALU.mult).then_inc(yg_ready, 1)
                e.wait_ge(yg_ready, h + 1)
            for m in range(NM):
                e.wait_ge(piece_filled, 14 + m)
                e.tensor_tensor(out_i[:, m, :], psum_ab[(13 + m) % 2][:, :], gate_out[m], ALU.mult).then_inc(piece_freed, 1)
            e.wait_ge(piece_filled, 16)
            e.wait_ge(x_scaled, 1)
            e.tensor_tensor(x1, psum_ab[15 % 2][:, :], x_tok, ALU.add).then_inc(x1_ready, 1)
            e.wait_ge(x1_ready, 1)
        QT = NT
        GROUPS = []
        for c in range(NC):
            for j in range(0, 4 * c, 2):
                GROUPS.append((c, [(j, CW, 0, 0), (j + 1, CW, CW, 0)]))
            if c == 0:
                GROUPS += [(0, [(0, CW, 0, P), (1, CW, CW, 2 * P)]), (0, [(2, CW, 0, 3 * P), (3, CW, CW, 4 * P)])]
            else:
                GROUPS += [(c, [(4 * c, 4 * P, 0, P), (4 * c + 1, 3 * P, CW, P)]),
                           (c, [(4 * c + 2, 2 * P, 0, P), (4 * c + 3, P, 2 * P, P)])]
        NG = len(GROUPS)
        NP = NG // 2
        LAST = [max(g for g in range(NG) if GROUPS[g][0] == c) for c in range(NC)]
        FIRST = [min(g for g in range(NG) if GROUPS[g][0] == c) for c in range(NC)]
        MAX_PIECES = [(i, c) for i in range(QT) for c in range(i // 4 + 1)]
        NB = 3

        AHEAD_MAX = 16

        def step_order(maxima=True, early=True, scores=True):
            order = []
            queue = [("max", n, 1) for n in range(AHEAD_MAX, len(MAX_PIECES))] if maxima else []
            found = len(queue)
            queue += [("max", n, 2) for n in range(AHEAD_MAX)] if early else []
            if maxima:
                queue.insert(min(found + 3, len(queue)), ("maxrow", 0, 1))
            for t in range(NG):
                g = t + 2
                if g < NG or scores:
                    order.append(("scores", g % NG, g // NG))
                if t < NG - 1:
                    order += queue[0:2]
                    del queue[0:2]
                if t % 2:
                    order.append(("context", t // 2, 0))
                    for c in range(NC - 1):
                        if t // 2 == LAST[c] // 2 + 1:
                            order.append(("turn", c, 0))
            return order + queue + [("turn", NC - 1, 0)]

        def ring_of(order):
            return [x for x in order if x[0] in ("max", "maxrow", "turn")]

        ORDER = step_order()
        RING = ring_of(ORDER)
        NR = len(RING)
        assert NR % NB == 0
        ORDERS = {NH - 2: step_order(early=False), NH - 1: step_order(maxima=False, early=False, scores=False)}
        RINGS = {h: ring_of(ORDERS[h]) for h in ORDERS}
        FIRST_RING = ([("max", n, 1) for n in range(len(MAX_PIECES))] + [("max", n, 2) for n in range(3)] + [("maxrow", 0, 1)]
                      + [("max", n, 2) for n in range(3, AHEAD_MAX)])
        AHEAD = 2 * NR - len(FIRST_RING)

        def first_piece(h):
            if isinstance(h, int) and h < 0:
                return AHEAD
            if isinstance(h, int) and h == NH - 1:
                return NR * NH + len(RINGS[NH - 2])
            return (h + 2) * NR

        def ring_order(h):
            return RINGS.get(h, RING) if isinstance(h, int) else RING

        def turned(h, c):
            return first_piece(h) + ring_order(h).index(("turn", c, 0)) + 1

        def phase(h):
            return first_piece(h) % NB if isinstance(h, int) else 0

        def loaded(count, pair, h, b, ahead):
            return count * (((h + ahead) // 2 if pair is None else pair + (b + ahead) // 2) + 1)

        class Attention:
            pass

        def attention(L, x_in, w_cols, wt_raw, out_slot):
            s = Attention()
            s.x_ready = sem(f"att{L}_x_ready")
            s.xT_filled = sem(f"att{L}_xT_filled")
            s.xT_read = sem(f"att{L}_xT_read")
            s.qkv_filled = sem(f"att{L}_qkv_filled")
            s.qkv_read = sem(f"att{L}_qkv_read")
            s.qk_split = sem(f"att{L}_qk_split")
            s.parts_stored = sem(f"att{L}_parts_stored")
            s.ring_filled = sem(f"att{L}_ring_filled")
            s.ring_freed = sem(f"att{L}_ring_freed")
            s.scores_filled = sem(f"att{L}_scores_filled")
            s.exp_done = sem(f"att{L}_exp_done")
            s.context_done = sem(f"att{L}_context_done")
            s.context_read = sem(f"att{L}_context_read")
            s.maxrow_split = sem(f"att{L}_maxrow_split")
            s.maxrow_turned = sem(f"att{L}_maxrow_turned")
            s.value_staged = sem(f"att{L}_value_staged")
            s.staging_set = sem(f"att{L}_staging_set")
            s.weights_turned = sem(f"att{L}_weights_turned")
            s.weights_read = sem(f"att{L}_weights_read")
            s.ctx_turned = sem(f"att{L}_ctx_turned")
            s.ctx_read = sem(f"att{L}_ctx_read")
            s.out_filled = sem(f"att{L}_out_filled")
            s.ones_set = sem(f"att{L}_ones_set")
            s.split_step = sem(f"att{L}_split_step")
            s.recip_ready = sem(f"att{L}_recip_ready")
            s.maxrow_stored = sem(f"att{L}_maxrow_stored")
            s.m_loaded = [sem(f"att{L}_m_loaded{b}") for b in range(2)]
            s.e_loaded = [sem(f"att{L}_e_loaded{b}") for b in range(2)]
            s.maxrow_loaded = [sem(f"att{L}_maxrow_loaded{b}") for b in range(2)]
            s.q_dram = nc.dram_tensor(f"q_parts{L}", [NH, 3, HD, T], BF16).ap()
            s.k_dram = nc.dram_tensor(f"k_parts{L}", [NH, 5, HD, T], BF16).ap()
            s.m_dram = nc.dram_tensor(f"max_rows{L}", [2, 3 * QT, P], BF16).ap()
            s.xn, s.xT = x_in, slot(3)
            s.q_parts = arena[:, 4:6, :].rearrange("p a n -> p (a n)").bitcast(BF16).rearrange("p (i n) -> p i n", i=4)
            s.k_parts = arena[:, 6:8, :].rearrange("p a n -> p (a n)").bitcast(BF16).rearrange("p (i n) -> p i n", i=4)
            s.full, s.rest = slot(8), slot(9)
            s.v = slot(10)
            s.ctx, s.ctxT = slot(11), slot(3)
            s.mq, s.mk, s.eq, s.ek = (slot(12 + i).bitcast(BF16).rearrange("p (b n) -> p b n", b=2) for i in range(4))
            s.pt = pair(16).rearrange("p a n -> p (a n)").rearrange("p (b n) -> p b n", b=4)
            s.vs = extra[:, 0:1024].rearrange("p (b t c) -> p b t c", b=2, c=32)
            s.oe = extra[:, 1024:2048].rearrange("p (b n) -> p b n", b=2)
            s.mpart = extra[:, 2048:2112].rearrange("p (t c) -> p t c", c=4)
            s.mneg = extra[:, 2112:2128]
            s.mrest = extra[:, 2128:2144]
            s.mparts = extra[:, 2320:2384].bitcast(BF16)
            s.mrow = extra[0:48, 2176:2304].bitcast(BF16).rearrange("p (b n) -> p b n", b=2)
            s.recip = extra[:, 2304:2312].rearrange("p (b t) -> p b t", b=2)
            s.w = w_cols
            s.wt_raw = wt_raw
            s.L = L
            s.out_slot = out_slot
            return s

        def ring(n):
            return psum_b[:, (n % NB) * CW:(n % NB + 1) * CW]
        context_bank = psum_b[:, NB * CW:(NB + 1) * CW]

        def att_sync(e, s):
            e.wait_ge(s.qk_split, 1)
            for i in range(3):
                e.dma_start(s.q_dram[:, i, :, :],
                            s.q_parts[:, i, :]).then_inc(s.parts_stored, 16)
            e.wait_ge(s.qk_split, 2)
            for i in range(5):
                e.dma_start(s.k_dram[:, i, :, :], s.k_parts[:, i % 3, :]).then_inc(s.parts_stored, 16)
            e.wait_ge(s.parts_stored, 8 * 16)
            e.wait_ge(s.ones_set, 1)

            def load(q, k, h, b, done):
                for r in range(3):
                    e.dma_start(q[24 * r:24 * r + 24, b, :],
                                s.q_dram[bass.ds(h, 1), :, :, :].rearrange("a i d t -> (a i d) t")).then_inc(done, 16)
                    e.dma_start(k[24 * r:24 * r + 24, b, :],
                                s.k_dram[bass.ds(h, 1), r:r + 3, :, :].rearrange("a i d t -> (a i d) t")).then_inc(done, 16)

            def maxrow(h, b):
                e.wait_ge(s.maxrow_turned, h + 1)
                e.dma_start(s.m_dram[b, :, :], s.mrow[:, b, :]).then_inc(s.maxrow_stored, 16)
                e.wait_ge(s.maxrow_stored, 16 * (h + 1))
                e.dma_start(s.eq[ROWS:ROWS + 3, b, :], s.m_dram[b, :, :].rearrange("(i t) p -> i (t p)", i=3)).then_inc(s.maxrow_loaded[b], 16)

            def step(h, b, load_max=True):
                e.wait_ge(s.context_done, NP * h + 2)
                load(s.eq, s.ek, h + 1, 1 - b, s.e_loaded[1 - b])
                maxrow(h + 1, 1 - b)
                if load_max:
                    load(s.mq, s.mk, h + 3, 1 - b, s.m_loaded[1 - b])

            load(s.mq, s.mk, 0, 0, s.m_loaded[0])
            load(s.mq, s.mk, 1, 1, s.m_loaded[1])
            load(s.eq, s.ek, 0, 0, s.e_loaded[0])
            maxrow(0, 0)
            load(s.mq, s.mk, 2, 0, s.m_loaded[0])
            with e.Fori(0, NH // 2 - 2) as i:
                step(2 * i, 0)
                step(2 * i + 1, 1)
            for h in range(NH - 4, NH - 1):
                step(h, h % 2, load_max=h + 3 < NH)

        def att_pool(e, s):
            e.wait_ge(s.xT_read, 1)
            e.memset(s.ek[64:ROWS + 3, :, :], 1.0).then_inc(s.ones_set, 1)
            e.wait_ge(s.ones_set, 1)
            e.memset(s.vs[:, :, :, HD + 1:32], 0.0).then_inc(s.staging_set, 1)
            e.memset(s.vs[:, :, :, HD:HD + 1], 1.0).then_inc(s.staging_set, 1)
            e.wait_ge(s.qkv_read, 3)

            def stage(h, b):
                e.tensor_copy(s.vs[:, b, :, 0:HD], tiled(s.v)[:, :, bass.ds(h * HD, HD)]).then_inc(s.value_staged, 1)

            def later(h, b):
                e.wait_ge(s.context_done, NP * (h - 1) + 2)
                stage(h, b)
            stage(0, 0)
            stage(1, 1)
            with e.Fori(1, NH // 2) as i:
                later(2 * i, 0)
                later(2 * i + 1, 1)

        def att_pe(e, s):
            e.wait_ge(s.x_ready, 1)
            if s.wt_raw is not None:
                for i in range(4):
                    t = e.transpose(psum_b[:, i * P:(i + 1) * P], s.wt_raw[:, i, :], ident[:, :])
                t.then_inc(s.weights_turned, 1)
                e.wait_ge(s.weights_read, 1)
            for t in range(NT):
                i = e.transpose(psum_a[:, t * P:(t + 1) * P], s.xn[:, t * P:(t + 1) * P], ident[:, :])
            i.then_inc(s.xT_filled, 1)
            e.wait_ge(s.xT_read, 1)
            for n in range(2):
                for c in range(NC):
                    i = e.matmul(psum_ab[1 - n][:, c * CW:(c + 1) * CW], s.w[:, n, :], s.xT[:, c * CW:(c + 1) * CW], start=True, stop=True)
                i.then_inc(s.qkv_filled, 1)
            e.wait_ge(s.qkv_read, 1)
            for t in range(NT):
                i = e.matmul(psum_b[:, t * P:(t + 1) * P], s.xT[:, t * P:(t + 1) * P], s.w[:, 2, :], start=True, stop=True)
            i.then_inc(s.qkv_filled, 1)
            e.wait_ge(s.qkv_read, 3)
            e.sem_inc(s.ring_filled, AHEAD)
            e.sem_inc(s.context_done, 2)

            def ring_wait(at):
                e.wait_ge(s.ring_freed, at - NB + 1)

            def ring_piece(h, b, n, x):
                ps, kind, k = ring(n), x[0], x[1]
                if kind == "max":
                    i, c = MAX_PIECES[k]
                    width = min(CW, (i + 1) * P - c * CW)
                    diagonal = c == i // 4
                    m = e.matmul(ps[:, 0:width], s.mq[0:ROWS, b, i * P:(i + 1) * P], s.mk[0:ROWS, b, c * CW:c * CW + width],
                                 start=True, stop=not diagonal)
                    if diagonal:
                        m = e.matmul(ps[:, width - P:width], ident_bf[:, :], mask_q[:, :], start=False, stop=True)
                else:
                    e.wait_ge(s.maxrow_split, h + 1)
                    m = e.transpose(ps[:, 0:64].bitcast(BF16), s.mparts[:, :], ident_bf[:, :])
                m.then_inc(s.ring_filled, 1)


            def scores_group(h, b, g):
                c, blocks = GROUPS[g]
                e.wait_ge(s.exp_done, NG * h + g + 1)
                for j, width, at, masked in blocks:
                    ps = psum_a[:, (g % 2) * HALF + at:(g % 2) * HALF + at + width]
                    m = e.matmul(ps, s.ek[0:ROWS + 3, b, j * P:(j + 1) * P], s.eq[0:ROWS + 3, b, (c + 1) * CW - width:(c + 1) * CW],
                                 start=True, stop=not masked)
                    if masked:
                        m = e.matmul(ps[:, 0:masked], ident_bf[:, :], mask_k[:, CW - masked:CW], start=False, stop=True)
                m.then_inc(s.scores_filled, 1)

            def context(h, b, p):
                c = GROUPS[2 * p][0]
                e.wait_ge(s.exp_done, NG * h + 2 * p + 4)
                if 2 * p == FIRST[c]:
                    e.wait_ge(s.context_read, NC * h + c + 1)
                for g in (2 * p, 2 * p + 1):
                    for j, width, at, masked in GROUPS[g][1]:
                        k = j % 4
                        m = e.matmul(context_bank[32 * k:32 * k + 32, CW - width:CW], s.vs[:, b, j, :], s.pt[:, g % 4, at:at + width],
                                     start=(j < 4), stop=(j >= 4 * c), skip_group_check=True)
                m.then_inc(s.context_done, 1)

            def turn(h, c, n):
                e.wait_ge(s.context_read, NC * h + c + 2)
                for t in range(4):
                    m = e.matmul(ring(n)[:, 16 * t:16 * t + HD + 1], s.oe[:, c % 2, t * P:(t + 1) * P], sum_groups[:, :],
                                 start=True, stop=True)
                m.then_inc(s.ring_filled, 1)

            def step(h, b, pair=None, order=ORDER):
                idx = 0
                for x in order:
                    kind, k, ahead = x
                    if kind == "scores":
                        if ahead and k == 0:
                            e.wait_ge(s.e_loaded[1 - b], loaded(96, pair, h, b, 1))
                            e.wait_ge(s.maxrow_loaded[1 - b], loaded(16, pair, h, b, 1))
                        scores_group(h + ahead, (b + ahead) % 2, k)
                    elif kind == "context":
                        if k == 0:
                            e.wait_ge(s.value_staged, h + 1)
                        context(h, b, k)
                    else:
                        if kind == "max" and ahead == 2 and k == 0:
                            e.wait_ge(s.m_loaded[b], loaded(96, pair, h, b, 2))
                        ring_wait(first_piece(h) + idx)
                        if kind == "turn":
                            turn(h, k, phase(h) + idx)
                        else:
                            ring_piece(h + ahead, (b + ahead) % 2, phase(h) + idx, x)
                        idx += 1

            e.wait_ge(s.m_loaded[0], 96)
            for k, x in enumerate(FIRST_RING):
                if x == ("max", 0, 2):
                    e.wait_ge(s.m_loaded[1], 96)
                ring_wait(AHEAD + k)
                ring_piece(x[2] - 1, (x[2] - 1) % 2, AHEAD + k, x)
            e.wait_ge(s.e_loaded[0], 96)
            e.wait_ge(s.maxrow_loaded[0], 16)
            scores_group(0, 0, 0)
            scores_group(0, 0, 1)
            with e.Fori(0, NH // 2 - 1) as i:
                step(2 * i, 0, pair=i)
                step(2 * i + 1, 1, pair=i)
            step(NH - 2, 0, order=ORDERS[NH - 2])
            step(NH - 1, 1, order=ORDERS[NH - 1])

            e.wait_ge(s.ring_freed, first_piece(NH - 1) + NC)
            for t in range(NT):
                i = e.transpose(psum_a[:, t * P:(t + 1) * P], s.ctx[:, t * P:(t + 1) * P], ident[:, :])
            i.then_inc(s.ctx_turned, 1)
            e.wait_ge(s.ctx_read, 1)
            for t in range(NT):
                i = e.matmul(psum_b[:, t * P:(t + 1) * P], s.ctxT[:, t * P:(t + 1) * P], s.w[:, 3, :], start=True, stop=True)
            i.then_inc(s.out_filled, 1)

        def att_act(e, s):
            if s.wt_raw is not None:
                e.wait_ge(s.weights_turned, 1)
                e.activation(s.w[:, :, :].rearrange("p a n -> p (a n)"), psum_b[:, 0:4 * P], ACT.Copy).then_inc(s.weights_read, 1)
            e.wait_ge(s.xT_filled, 1)
            e.activation(s.xT, psum_a[:, :], ACT.Copy).then_inc(s.xT_read, 1)
            e.wait_ge(s.qkv_read, 3)
            e.sem_inc(s.exp_done, 2)
            e.sem_inc(s.context_read, 1)

            def read_context(h, c):
                e.wait_ge(s.context_done, NP * h + LAST[c] // 2 + 3)
                e.wait_ge(s.ring_filled, turned(h, c - 2) if c >= 2 else turned(h - 1, c + 2))
                e.activation(s.oe[:, c % 2, :], context_bank, ACT.Copy).then_inc(s.context_read, 1)

            def exp_group(h, g):
                width = sum(w for _, w, _, _ in GROUPS[g][1])
                e.wait_ge(s.scores_filled, NG * h + g + 1)
                e.wait_ge(s.context_done, NP * h + g // 2 + 1)
                e.activation(s.pt[:, g % 4, 0:width], psum_a[:, (g % 2) * HALF:(g % 2) * HALF + width], ACT.Exp).then_inc(s.exp_done, 1)

            def step(h, last=False):
                for g in range(2, NG + 2):
                    if g < NG or not last:
                        exp_group(h + g // NG, g % NG)
                    for c in range(NC):
                        if g == LAST[c] + 2:
                            read_context(h, c)

            exp_group(0, 0)
            exp_group(0, 1)
            with e.Fori(0, NH // 2 - 1) as i:
                step(2 * i)
                step(2 * i + 1)
            step(NH - 2)
            step(NH - 1, last=True)
            e.wait_ge(s.ctx_turned, 1)
            e.activation(s.ctxT, psum_a[:, :], ACT.Copy).then_inc(s.ctx_read, 1)

        def att_dve(e, s, finish):
            for n, (parts, bias) in enumerate(((s.q_parts, q_b), (s.k_parts, k_b))):
                e.wait_ge(s.qkv_filled, n + 1)
                scale = SCORE_SCALE if n == 0 else 1.0
                if s.L == 0:
                    i = e.tensor_scalar(s.full, psum_ab[1 - n][:, :], bias, scale, ALU.add, ALU.mult)
                else:
                    i = e.tensor_scalar(s.full, psum_ab[1 - n][:, :], scale, None, ALU.mult)
                i.then_inc(s.qkv_read, 1)
                e.wait_ge(s.qkv_read, n + 1)
                dve_link(e, e.tensor_copy(parts[:, 0, :], s.full))
                dve_link(e, e.tensor_tensor(s.rest, s.full, parts[:, 0, :], ALU.subtract))
                dve_link(e, e.tensor_copy(parts[:, 1, :], s.rest))
                e.tensor_tensor(parts[:, 2, :], s.rest, parts[:, 1, :], ALU.subtract).then_inc(s.qk_split, 1)
                e.wait_ge(s.qk_split, n + 1)
            e.wait_ge(s.qkv_filled, 3)
            if s.L == 0:
                e.tensor_tensor(tiled(s.v), tiled(psum_b[:, :]), v_b_row.unsqueeze(1).to_broadcast([P, NT, D]), ALU.add).then_inc(s.qkv_read, 1)
            else:
                e.tensor_copy(s.v, psum_b[:, :]).then_inc(s.qkv_read, 1)
            dve_link(e, e.memset(s.mpart, NEG))
            dve_link(e, e.memset(s.mparts, 0.0))
            e.sem_inc(s.ring_freed, AHEAD)

            def link(h, k, ins):
                ins.then_inc(s.split_step, 1)
                e.wait_ge(s.split_step, 4 * h + k + 1)

            def ring_read(step, b, idx, x):
                ps, h, number = ring(phase(step) + idx), step + x[2], first_piece(step) + idx
                e.wait_ge(s.ring_filled, number + 1)
                if x[0] == "max":
                    i, c = MAX_PIECES[x[1]]
                    width = min(CW, (i + 1) * P - c * CW)
                    e.tensor_reduce(s.mpart[:, i, c:c + 1], ps[:, 0:width], AX.X, ALU.max).then_inc(s.ring_freed, 1)
                    if x[1] == len(MAX_PIECES) - 1:
                        e.wait_ge(s.ring_freed, number + 1)
                        link(h, 0, e.tensor_reduce(s.mneg, s.mpart, AX.X, ALU.max, negate=True))
                        link(h, 1, e.tensor_copy(s.mparts[:, 0:16], s.mneg))
                        link(h, 2, e.tensor_tensor(s.mrest, s.mneg, s.mparts[:, 0:16], ALU.subtract))
                        link(h, 3, e.tensor_copy(s.mparts[:, 16:32], s.mrest))
                        e.tensor_tensor(s.mparts[:, 32:48], s.mrest, s.mparts[:, 16:32], ALU.subtract).then_inc(s.maxrow_split, 1)
                elif x[0] == "maxrow":
                    e.tensor_copy(s.mrow[:, (b + 1) % 2, :], ps[0:48, 0:64].bitcast(BF16)).then_inc(s.maxrow_turned, 1)
                    e.wait_ge(s.maxrow_turned, h + 1)
                    e.sem_inc(s.ring_freed, 1)
                else:
                    c = x[1]
                    got = ps[:, 0:64].rearrange("p (t k) -> p t k", k=16)
                    e.reciprocal(s.recip[:, c % 2, :], got[:, :, HD]).then_inc(s.recip_ready, 1)
                    e.wait_ge(s.recip_ready, NC * h + c + 1)
                    e.tensor_tensor(tiled(s.ctx)[:, 4 * c:4 * c + 4, bass.ds(h * HD, HD)], got[:, :, 0:HD],
                                    s.recip[:, c % 2, :].unsqueeze(2).to_broadcast([P, 4, HD]), ALU.mult).then_inc(s.ring_freed, 1)

            def step(h, b):
                for idx, x in enumerate(ring_order(h)):
                    ring_read(h, b, idx, x)

            for k, x in enumerate(FIRST_RING):
                ring_read(-1, 1, k, x)
            with e.Fori(0, NH // 2 - 1) as i:
                step(2 * i, 0)
                step(2 * i + 1, 1)
            step(NH - 2, 0)
            step(NH - 1, 1)
            e.wait_ge(s.out_filled, 1)
            finish(e, s)

        hidden = slot(0)
        hidden2 = slot(2)
        att0 = attention(0, slot(2), w_att[0], None, slot(2))
        h_biased = sem("h_biased")
        ln1_scaled = sem("ln1_scaled")
        hidden2_ready = sem("hidden2_ready")
        ATT_LOADS = 16

        def attention_loads(e):
            names = ("q", "k", "v", "o")
            for i, n in enumerate(names):
                e.dma_start(w_att[0][:, i, :], a[f"L0_ffn_{n}_w"]).then_inc(attention_weights_loaded, 16)
                e.dma_start(w_raw[:, i, :], a[f"L1_attn_W{n}"]).then_inc(attention_weights_loaded, 16)
            for dst, src in ((q_b, "q_b"), (k_b, "k_b")):
                e.dma_start(dst, a[f"L0_ffn_{src}"].rearrange("(p a) -> p a", a=1)).then_inc(attention_weights_loaded, 16)
            for dst, src in ((ln1_w, "ln1_w"), (ln1_b, "ln1_b"), (v_b_row, "v_b"), (o_b_row, "o_b"), (ln2_w, "ln2_w"), (ln2_b, "ln2_b")):
                e.dma_start(dst, row_of(a[f"L0_ffn_{src}"])).then_inc(attention_weights_loaded, 16)

        def wide(row):
            return row.unsqueeze(1).to_broadcast([P, NT, D])

        def att0_before_dve(e):
            norm_dve(e, "ln_b", x1, hidden)
            norm_dve(e, "ln_b1", hidden, att0.xn)
            e.wait_ge(attention_weights_loaded, 16 * ATT_LOADS)
            dve_link(e, e.tensor_tensor(tiled(att0.xn), tiled(att0.xn), wide(ln1_w), ALU.mult))
            e.tensor_tensor(tiled(att0.xn), tiled(att0.xn), wide(ln1_b), ALU.add).then_inc(att0.x_ready, 1)

        def att0_before_pool(e):
            e.wait_ge(attention_weights_loaded, 16 * ATT_LOADS)
            e.wait_ge(tile_normed, normed("ln_b1"))
            e.tensor_tensor(tiled(hidden), tiled(hidden), wide(o_b_row), ALU.add).then_inc(h_biased, 1)
            e.wait_ge(h_biased, 1)

        def att0_finish(e, s):
            e.wait_ge(h_biased, 1)
            e.tensor_tensor(hidden2, psum_b[:, :], hidden, ALU.add).then_inc(hidden2_ready, 1)
            e.wait_ge(hidden2_ready, 1)

        def top_two(e, link, logits, picks, E, expert_ids, largest, second, spare, spare2, index):
            def wide_e(v):
                return v.unsqueeze(2).to_broadcast([P, NT, E])
            source = logits
            for k, value in enumerate((largest, second)):
                link(e, e.tensor_reduce(value, source, AX.X, ALU.max))
                link(e, e.tensor_tensor(spare, source, wide_e(value), ALU.is_equal))
                link(e, e.scalar_tensor_tensor(spare, spare, -64.0, expert_ids, ALU.mult, ALU.add))
                link(e, e.tensor_reduce(index, spare, AX.X, ALU.min))
                link(e, e.tensor_scalar(index, index, 64.0, None, ALU.add))
                link(e, e.tensor_tensor(picks[k], expert_ids, wide_e(index), ALU.is_equal))
                if k == 0:
                    link(e, e.scalar_tensor_tensor(spare2, picks[0], NEG, logits, ALU.mult, ALU.add))
                    source = spare2

        xt, xtT = slot(3), slot(4)
        fc1 = arena[:, 5, 0:2 * F0].rearrange("p (b f) -> p b f", b=2)
        fc2 = arena[:, 5, 2 * F0:4 * F0].rearrange("p (b k n) -> p b k n", b=2, n=D)
        KF = F0 // P
        ST = CAP // P
        x_exp = arena[:, 6, 0:2 * CAP].rearrange("p (b s d) -> p b s d", b=2, d=D)
        x_expT = arena[:, 6, 2 * CAP:4 * CAP].rearrange("p (b s) -> p b s", b=2)
        y_exp = arena[:, 6, 4 * CAP:6 * CAP].rearrange("p (b s d) -> p b s d", b=2, d=D)
        h_exp = arena[:, 7, :].rearrange("p (b k s) -> p b k s", b=2, k=KF)
        fc2_b = arena[0:1, 8, :]
        got = [slot(9), slot(10)]
        fc1_b_raw = arena[0:E0 * KF, 11, 0:P]
        fc1_b = arena[:, 11, P:P + E0 * KF]
        router_w = arena[:, 11, 256:256 + E0]
        small = arena[:, 12:14, :].rearrange("p a n -> p (a n)")

        def cut(at, n):
            return small[:, at:at + n]

        def by_expert(v, E=E0):
            return v.rearrange("p (t e) -> p t e", e=E)
        logits, expert_ids, spare, spare2, probs = (by_expert(cut(256 * i, 256)) for i in range(5))
        picks = cut(1280, 512).rearrange("p (t s e) -> p t s e", s=2, e=E0)
        picks_bf = cut(1792, 256).bitcast(BF16)
        place = cut(2048, 512).rearrange("p (t s e) -> p t s e", s=2, e=E0)
        before = cut(2560, 512).rearrange("p (t s e) -> p t s e", s=2, e=E0)
        largest, second, index, total, = (cut(3072 + 16 * i, 16) for i in range(4))
        slot_of, kept, gates, dump_row, to_scatter, to_gather = (cut(3136 + 32 * i, 32).rearrange("p (t s) -> p t s", s=2) for i in range(6))
        ids_int = cut(3328, 256).bitcast(I32)
        dump_int = cut(3584, 32).bitcast(I32)
        scatter_int, gather_int = (cut(3616 + 32 * i, 32).bitcast(I32) for i in range(2))
        zeros = sb("zeros", [P, 1024])

        DUMP = SLOTS
        xin_dram = nc.dram_tensor("expert_inputs", [SLOTS + 2 * T, D], F32).ap()
        eout_dram = nc.dram_tensor("expert_outputs", [SLOTS + P, D], F32).ap()

        zeros_set, dram_zeroed = sem("zeros_set"), sem("dram_zeroed")
        moe_loaded = sem("moe_loaded")
        xt_ready, xtT_filled, xtT_read = sem("xt_ready"), sem("xtT_filled"), sem("xtT_read")
        logits_filled, picks_ready, places_filled, routed = sem("logits_filled"), sem("picks_ready"), sem("places_filled"), sem("routed")
        moe_iota, fc1_b_read = sem("moe_iota"), sem("fc1_b_read")
        shifted_ready, exp_ready = sem("shifted_ready"), sem("exp_ready")
        scattered, gathered = sem("scattered"), sem("gathered")
        fc_loaded = [sem(f"fc_loaded{b}") for b in range(2)]
        x_exp_loaded = [sem(f"x_exp_loaded{b}") for b in range(2)]
        x_exp_turned, x_exp_read, h_filled, h_ready, y_filled, y_exp_ready = (
            sem(n) for n in ("x_exp_turned", "x_exp_read", "h_filled", "h_ready", "y_filled", "y_exp_ready"))
        y_exp_stored = [sem(f"y_exp_stored{b}") for b in range(2)]
        x12_ready, x2_ready = sem("x12_ready"), sem("x2_ready")
        combined = sem("combined")
        x2 = slot(1)

        def moe0_zero(e):
            e.wait_ge(zeros_set, 1)
            rows_each = 1024 // D
            for i in range(SLOTS // (P * rows_each)):
                e.dma_start(xin_dram[i * P * rows_each:(i + 1) * P * rows_each, :].rearrange("(p r) d -> p (r d)", p=P),
                            zeros[:, :]).then_inc(dram_zeroed, 16)
            e.dma_start(eout_dram[SLOTS:SLOTS + P, :], zeros[:, 0:D]).then_inc(dram_zeroed, 16)
        ZEROED = 16 * (SLOTS // (P * 8) + 1)

        def moe0_sync(e):
            e.wait_ge(hidden2_ready, 1)
            e.dma_start(fc2_b, a["L0_ffn_fc2_b"].rearrange("(a e) n -> a (e n)", a=1)).then_inc(moe_loaded, 16)
            e.dma_start(fc1_b_raw, a["L0_ffn_fc1_b"].rearrange("e (k p) -> (e k) p", p=P)).then_inc(moe_loaded, 16)
            e.dma_start(router_w, a["L0_ffn_router_w"]).then_inc(moe_loaded, 16)

            def weights(x, b):
                e.dma_start(fc1[:, b, :], a["L0_ffn_fc1_w"][bass.ds(x, 1), :, :].rearrange("a d f -> (a d) f")).then_inc(fc_loaded[b], 16)
                e.dma_start(fc2[:, b, :, :], a["L0_ffn_fc2_w"][bass.ds(x, 1), :, :].rearrange("a (k p) n -> p (a k) n", p=P)).then_inc(fc_loaded[b], 16)

            def inputs(x, b):
                e.dma_start(x_exp[:, b, :, :], xin_dram[bass.ds(x * CAP, CAP), :].rearrange("(s p) d -> p s d", p=P)).then_inc(x_exp_loaded[b], 16)

            def store(x, b):
                e.wait_ge(y_exp_ready, x + 1)
                e.dma_start(eout_dram[bass.ds(x * CAP, CAP), :].rearrange("(s p) d -> p s d", p=P), y_exp[:, b, :, :]).then_inc(y_exp_stored[b], 16)

            for b in range(2):
                weights(b, b)
            e.wait_ge(scattered, 16 * 2 * NT)
            for b in range(2):
                inputs(b, b)

            def follow(x, b, more=True):
                if more:
                    e.wait_ge(x_exp_read, x + 1)
                    inputs(x + 2, b)
                store(x, b)
                if more:
                    weights(x + 2, b)
            with e.Fori(0, E0 // 2 - 1) as i:
                follow(2 * i, 0)
                follow(2 * i + 1, 1)
            follow(E0 - 2, 0, more=False)
            follow(E0 - 1, 1, more=False)

        def moe0_pool(e):
            e.wait_ge(hidden2_ready, 1)
            e.tensor_tensor(x2, x1, hidden2, ALU.add).then_inc(x12_ready, 1)
            e.wait_ge(x12_ready, 1)
            e.iota(ids_int, pattern=[[0, NT], [1, E0]], base=0, channel_multiplier=0).then_inc(moe_iota, 1)
            e.iota(dump_int, pattern=[[P, NT], [T, 2]], base=DUMP, channel_multiplier=1).then_inc(moe_iota, 1)
            e.wait_ge(routed, 1)
            e.wait_ge(dram_zeroed, ZEROED)
            for t in range(NT):
                for k in range(2):
                    e.indirect_dma_start(out=xin_dram, out_offset=bass.IndirectOffsetOnAxis(ap=scatter_int[:, 2 * t + k:2 * t + k + 1], axis=0),
                                         in_=xt[:, t * D:(t + 1) * D], in_offset=None).then_inc(scattered, 16)
            for b in range(2):
                e.wait_ge(y_exp_stored[b], 16 * E0 // 2)
            for t in range(NT):
                for k in range(2):
                    e.indirect_dma_start(out=got[k][:, t * D:(t + 1) * D], out_offset=None, in_=eout_dram,
                                         in_offset=bass.IndirectOffsetOnAxis(ap=gather_int[:, 2 * t + k:2 * t + k + 1], axis=0)).then_inc(gathered, 16)

        def moe0_pe(e):
            e.wait_ge(xt_ready, 1)
            for t in range(NT):
                i = e.transpose(psum_a[:, t * P:(t + 1) * P], xt[:, t * P:(t + 1) * P], ident[:, :])
            i.then_inc(xtT_filled, 1)
            e.wait_ge(moe_loaded, 48)
            e.transpose(psum_b[:, CW:CW + E0 * KF], fc1_b_raw, ident[0:E0 * KF, 0:E0 * KF])
            e.wait_ge(xtT_read, 1)
            for t in range(NT):
                i = e.matmul(psum_b[:, t * E0:(t + 1) * E0], xtT[:, t * P:(t + 1) * P], router_w, start=True, stop=True)
            i.then_inc(logits_filled, 1)
            e.wait_ge(picks_ready, 1)
            e.matmul(psum_a[:, 0:CW], tri_bf[:, :], picks_bf, start=True, stop=True)
            e.matmul(psum_a[:, CW:2 * CW], ones_bf[:, :], picks_bf, start=True, stop=True).then_inc(places_filled, 1)
            e.wait_ge(routed, 1)

            def up(x, pair, b, first=False):
                ps = psum_ab[b]
                e.wait_ge(x_exp_loaded[b], 16 * (pair + 1))
                for s in range(ST):
                    i = e.transpose(ps[:, s * P:(s + 1) * P], x_exp[:, b, s, :], ident[:, :])
                i.then_inc(x_exp_turned, 1)
                e.wait_ge(fc_loaded[b], 32 * (pair + 1))
                e.wait_ge(x_exp_read, x + 1)
                for k in range(KF):
                    i = e.matmul(ps[:, CW + k * CAP:CW + (k + 1) * CAP], fc1[:, b, k * P:(k + 1) * P], x_expT[:, b, :], start=True, stop=True)
                i.then_inc(h_filled, 1)

            def down(x, b):
                ps = psum_ab[b]
                e.wait_ge(h_ready, x + 1)
                for s in range(ST):
                    o = ps[:, 3 * CW + s * P:3 * CW + (s + 1) * P]
                    e.matmul(o, ones_row[:, :], fc2_b[:, ds(x, D)], start=True, stop=False)
                    for k in range(KF):
                        i = e.matmul(o, h_exp[:, b, k, s * P:(s + 1) * P], fc2[:, b, k, :], start=False, stop=(k == KF - 1))
                i.then_inc(y_filled, 1)

            with e.Fori(0, E0 // 2) as i:
                up(2 * i, i, 0)
                up(2 * i + 1, i, 1)
                down(2 * i, 0)
                down(2 * i + 1, 1)

        def moe0_act(e):
            norm_act(e, "ln_b2")
            e.wait_ge(xtT_filled, 1)
            e.activation(xtT, psum_a[:, :], ACT.Copy).then_inc(xtT_read, 1)
            e.wait_ge(logits_filled, 1)
            e.activation(fc1_b, psum_b[:, CW:CW + E0 * KF], ACT.Copy).then_inc(fc1_b_read, 1)
            e.wait_ge(shifted_ready, 1)
            e.activation(probs, probs, ACT.Exp).then_inc(exp_ready, 1)
            e.wait_ge(fc1_b_read, 1)

            def hidden_units(x, b):
                e.wait_ge(h_filled, x + 1)
                for k in range(KF):
                    i = e.activation(h_exp[:, b, k, :], psum_ab[b][:, CW + k * CAP:CW + (k + 1) * CAP], ACT.Gelu,
                                     bias=fc1_b[:, bass.ds(x * KF + k, 1)])
                i.then_inc(h_ready, 1)
            with e.Fori(0, E0 // 2) as i:
                hidden_units(2 * i, 0)
                hidden_units(2 * i + 1, 1)

        def moe0_dve(e):
            norm_dve(e, "ln_b2", hidden2, xt)
            dve_link(e, e.tensor_tensor(tiled(xt), tiled(xt), wide(ln2_w), ALU.mult))
            e.tensor_tensor(tiled(xt), tiled(xt), wide(ln2_b), ALU.add).then_inc(xt_ready, 1)
            e.wait_ge(moe_iota, 2)
            dve_link(e, e.tensor_copy(expert_ids, by_expert(ids_int)))
            dve_link(e, e.tensor_copy(dump_row, dump_int.rearrange("p (t s) -> p t s", s=2)))
            e.wait_ge(logits_filled, 1)
            dve_link(e, e.tensor_copy(logits, by_expert(psum_b[:, 0:NT * E0])))
            top_two(e, dve_link, logits, [picks[:, :, k, :] for k in range(2)], E0, expert_ids, largest, second, spare, spare2, index)
            e.tensor_copy(picks_bf, picks.rearrange("p t s e -> p (t s e)")).then_inc(picks_ready, 1)

            def wide_e(v):
                return v.unsqueeze(2).to_broadcast([P, NT, E0])
            e.tensor_tensor(probs, logits, wide_e(largest), ALU.subtract).then_inc(shifted_ready, 1)
            inclusive = psum_a[:, 0:CW].rearrange("p (t s e) -> p t s e", s=2, e=E0)
            totals = psum_a[:, CW:2 * CW].rearrange("p (t s e) -> p t s e", s=2, e=E0)
            dve_link(e, e.memset(before[:, 0, :, :], 0.0))
            e.wait_ge(places_filled, 1)
            for t in range(1, NT):
                dve_link(e, e.tensor_tensor(before[:, t, :, :], totals[:, t - 1, :, :], before[:, t - 1, :, :], ALU.add))
            dve_link(e, e.tensor_tensor(total, totals[:, NT - 1, 0, :], before[:, NT - 1, 0, :], ALU.add))
            dve_link(e, e.tensor_tensor(place, inclusive, before, ALU.add))
            dve_link(e, e.tensor_tensor(place[:, :, 1, :], place[:, :, 1, :], total.unsqueeze(1).to_broadcast([P, NT, E0]), ALU.add))
            flat = [v.rearrange("p t s e -> p (t s e)") for v in (place, picks)]
            dve_link(e, e.scalar_tensor_tensor(flat[1], flat[0], CAP + 0.5, flat[1], ALU.is_lt, ALU.mult))
            dve_link(e, e.tensor_reduce(kept, picks, AX.X, ALU.add))
            for k in range(2):
                dve_link(e, e.scalar_tensor_tensor(spare, expert_ids, float(CAP), place[:, :, k, :], ALU.mult, ALU.add))
                dve_link(e, e.scalar_tensor_tensor(spare, spare, -1.0, picks[:, :, k, :], ALU.add, ALU.mult))
                dve_link(e, e.tensor_reduce(slot_of[:, :, k], spare, AX.X, ALU.add))
            dve_link(e, e.tensor_tensor(to_scatter, kept, dump_row, ALU.mult))
            dve_link(e, e.tensor_tensor(to_scatter, dump_row, to_scatter, ALU.subtract))
            dve_link(e, e.tensor_tensor(to_scatter, to_scatter, slot_of, ALU.add))
            dve_link(e, e.tensor_scalar(to_gather, kept, -float(SLOTS), float(SLOTS), ALU.mult, ALU.add))
            dve_link(e, e.tensor_tensor(to_gather, to_gather, slot_of, ALU.add))
            dve_link(e, e.tensor_copy(gather_int, to_gather.rearrange("p t s -> p (t s)")))
            e.tensor_copy(scatter_int, to_scatter.rearrange("p t s -> p (t s)")).then_inc(routed, 1)
            e.wait_ge(exp_ready, 1)
            dve_link(e, e.tensor_reduce(index, probs, AX.X, ALU.add))
            dve_link(e, e.reciprocal(index, index))
            dve_link(e, e.tensor_tensor(probs, probs, wide_e(index), ALU.mult))
            for k in range(2):
                dve_link(e, e.tensor_tensor(spare, probs, picks[:, :, k, :], ALU.mult))
                dve_link(e, e.tensor_reduce(gates[:, :, k], spare, AX.X, ALU.add))
            dve_link(e, e.tensor_tensor(index, gates[:, :, 0], gates[:, :, 1], ALU.add))
            dve_link(e, e.tensor_scalar(index, index, 1.1920929e-07, None, ALU.max))
            dve_link(e, e.reciprocal(index, index))
            for k in range(2):
                dve_link(e, e.tensor_tensor(gates[:, :, k], gates[:, :, k], index, ALU.mult))

            def expert(x, pair, b):
                ps = psum_ab[b]
                e.wait_ge(x_exp_turned, x + 1)
                e.tensor_copy(x_expT[:, b, :], ps[:, 0:CAP]).then_inc(x_exp_read, 1)

            def outputs(x, pair, b, first=False):
                e.wait_ge(y_filled, x + 1)
                if not first:
                    e.wait_ge(y_exp_stored[b], 16 * pair)
                e.tensor_scalar(y_exp[:, b, :, :], psum_ab[b][:, 3 * CW:3 * CW + CAP].rearrange("p (s d) -> p s d", d=D),
                                1.0 - 0.2, None, ALU.mult).then_inc(y_exp_ready, 1)

            def both(i, first=False):
                expert(2 * i, i, 0)
                expert(2 * i + 1, i, 1)
                outputs(2 * i, i, 0, first)
                outputs(2 * i + 1, i, 1, first)
            both(0, first=True)
            with e.Fori(1, E0 // 2) as i:
                both(i)
            e.wait_ge(gathered, 16 * 2 * NT)
            for k in range(2):
                with e.Fori(0, NT) as t:
                    e.scalar_tensor_tensor(x2[:, ds(t, D)], got[k][:, ds(t, D)], gates[:, bass.ds(t, 1), k], x2[:, ds(t, D)],
                                           ALU.mult, ALU.add).then_inc(combined, 1)
                e.wait_ge(combined, NT * (k + 1))
            e.sem_inc(x2_ready, 1)

        x3 = slot(0)
        att1 = attention(1, slot(2), w_att[1], w_raw, slot(0))
        x3_ready = sem("x3_ready")

        def att1_before_dve(e):
            norm_dve(e, "ln_c", x2, att1.xn)
            e.sem_inc(att1.x_ready, 1)

        def att1_finish(e, s):
            e.tensor_tensor(x3, psum_b[:, :], x2, ALU.add).then_inc(x3_ready, 1)
            e.wait_ge(x3_ready, 1)

        xf, xfT = slot(2), slot(3)
        KH = F1 // P
        w_gate = arena[:, 5, 0:2 * F1].rearrange("p (b f) -> p b f", b=2)
        w_up = arena[:, 5, 2 * F1:4 * F1].rearrange("p (b f) -> p b f", b=2)
        w_down = arena[:, 5, 4 * F1:4 * F1 + 2 * KH * D].rearrange("p (b k n) -> p b k n", b=2, n=D)
        silu_g = arena[:, 6, :].rearrange("p (b n) -> p b n", b=2)
        prod = arena[:, 7, :].rearrange("p (b k n) -> p b k n", b=2, k=KH)
        router1_raw = arena[0:E1, 11, 0:P]
        router1_w = arena[:, 11, P:P + E1]
        router1_b = arena[:, 11, 2 * P:2 * P + E1]
        logits1, ids1, spare1, spare1b = (cut(128 * i, 128).rearrange("p (t e) -> p t e", e=E1) for i in range(4))
        picks1 = cut(512, 256).rearrange("p (s t e) -> p s t e", s=2, e=E1)
        weight1 = cut(768, NT * (E1 + 1)).rearrange("p (t e) -> p t e", e=E1 + 1)
        largest1, second1, index1, share1 = (cut(1024 + 16 * i, 16) for i in range(4))
        ids1_int = cut(1152, 128).bitcast(I32).rearrange("p (t e) -> p t e", e=E1)
        UNITS = (E1 + 1) * NC

        moe1_loaded, moe1_iota = sem("moe1_loaded"), sem("moe1_iota")
        xf_ready, xfT_filled, xfT_read = sem("xf_ready"), sem("xfT_filled"), sem("xfT_read")
        router1_turned, router1_read, logits1_filled = sem("router1_turned"), sem("router1_read"), sem("logits1_filled")
        gap_ready, gap_exp, weights1_ready = sem("gap_ready"), sem("gap_exp"), sem("weights1_ready")
        expert_loaded = [sem(f"expert_loaded{b}") for b in range(2)]
        units_filled, silu_ready, prod_ready, down_filled, unit_added = (
            sem(n) for n in ("units_filled", "silu_ready", "prod_ready", "down_filled", "unit_added"))

        def moe1_sync(e):
            e.wait_ge(x3_ready, 1)
            e.dma_start(router1_raw, a["L1_ffn_router_w"]).then_inc(moe1_loaded, 16)
            e.dma_start(router1_b, row_of(a["L1_ffn_experts_bias"])).then_inc(moe1_loaded, 16)

            def weights(names, x, b):
                gate, up, down = (a[f"L1_ffn_{n}"][bass.ds(x, 1), :, :] for n in names)
                e.dma_start(w_gate[:, b, :], gate.rearrange("a d f -> (a d) f")).then_inc(expert_loaded[b], 16)
                e.dma_start(w_up[:, b, :], up.rearrange("a d f -> (a d) f")).then_inc(expert_loaded[b], 16)
                e.dma_start(w_down[:, b, :, :], down.rearrange("a (k p) n -> p (a k) n", p=P)).then_inc(expert_loaded[b], 16)
            routed_names = ("w1", "w3", "w2")
            weights(routed_names, 0, 0)
            weights(routed_names, 1, 1)
            with e.Fori(0, E1 // 2 - 1) as i:
                for b in range(2):
                    e.wait_ge(down_filled, NC * (2 * i + b + 1))
                    weights(routed_names, 2 * i + b + 2, b)
            e.wait_ge(down_filled, NC * (E1 - 1))
            weights(("sw1", "sw3", "sw2"), 0, 0)

        def moe1_pool(e):
            e.wait_ge(x3_ready, 1)
            e.iota(ids1_int, pattern=[[0, NT], [1, E1]], base=0, channel_multiplier=0).then_inc(moe1_iota, 1)

        def moe1_pe(e):
            e.wait_ge(xf_ready, 1)
            for t in range(NT):
                i = e.transpose(psum_a[:, t * P:(t + 1) * P], xf[:, t * P:(t + 1) * P], ident[:, :])
            i.then_inc(xfT_filled, 1)
            e.wait_ge(moe1_loaded, 32)
            e.transpose(psum_b[:, CW:CW + E1], router1_raw, ident[0:E1, 0:E1]).then_inc(router1_turned, 1)
            e.wait_ge(router1_read, 1)
            e.wait_ge(xfT_read, 1)
            for t in range(NT):
                i = e.matmul(psum_b[:, t * E1:(t + 1) * E1], xfT[:, t * P:(t + 1) * P], router1_w, start=True, stop=True)
            i.then_inc(logits1_filled, 1)

            def gate_up(c, b, u, first):
                ps = psum_ab[c % 2]
                for m, w, k in ((1, w_up, 0), (1, w_up, 1), (0, w_gate, 1), (0, w_gate, 0)):
                    if (m, k) == (0, 0) and not first:
                        e.wait_ge(unit_added, u - 1)
                    i = e.matmul(ps[:, (KH * m + k) * CW:(KH * m + k + 1) * CW], w[:, b, k * P:(k + 1) * P],
                                 xfT[:, c * CW:(c + 1) * CW], start=True, stop=True)
                i.then_inc(units_filled, 1)

            def down(c, b, u):
                e.wait_ge(prod_ready, u + 1)
                for t in range(4):
                    for k in range(KH):
                        i = e.matmul(psum_ab[c % 2][:, t * P:(t + 1) * P], prod[:, c % 2, k, t * P:(t + 1) * P], w_down[:, b, k, :],
                                     start=(k == 0), stop=(k == KH - 1))
                i.then_inc(down_filled, 1)

            def next_unit(c, b, u, first=False):
                if c == 0:
                    e.wait_ge(expert_loaded[b], 48 * (next_unit.pair + 1))
                gate_up(c, b, u, first)

            e.wait_ge(weights1_ready, 1)
            next_unit.pair = 0
            next_unit(0, 0, 0, first=True)
            next_unit(1, 0, 1, first=True)
            down(0, 0, 0)
            next_unit(2, 0, 2)
            down(1, 0, 1)
            next_unit(3, 0, 3)
            down(2, 0, 2)
            next_unit.pair = 0
            next_unit(0, 1, 4)
            down(3, 0, 3)

            def expert_units(x, b, pair, nxt):
                for c in range(1, NC):
                    next_unit(c, b, NC * x + c)
                    down(c - 1, b, NC * x + c - 1)
                next_unit.pair = nxt
                next_unit(0, 1 - b, NC * (x + 1))
                down(NC - 1, b, NC * x + NC - 1)

            expert_units(1, 1, 0, 1)
            with e.Fori(1, E1 // 2) as i:
                expert_units(2 * i, 0, i, i)
                expert_units(2 * i + 1, 1, i, i + 1)
            for c in range(1, NC):
                next_unit(c, 0, NC * E1 + c)
                down(c - 1, 0, NC * E1 + c - 1)
            down(NC - 1, 0, UNITS - 1)

        def moe1_act(e):
            norm_act(e, "ln_d")
            e.wait_ge(xfT_filled, 1)
            e.activation(xfT, psum_a[:, :], ACT.Copy).then_inc(xfT_read, 1)
            e.wait_ge(router1_turned, 1)
            e.activation(router1_w, psum_b[:, CW:CW + E1], ACT.Copy).then_inc(router1_read, 1)
            e.wait_ge(gap_ready, 1)
            e.activation(share1, share1, ACT.Exp).then_inc(gap_exp, 1)

            def unit(c, u, first=False):
                e.wait_ge(units_filled, u + 1)
                if not first:
                    e.wait_ge(prod_ready, u - 1)
                e.activation(silu_g[:, c % 2, :], psum_ab[c % 2][:, 0:KH * CW], ACT.Silu).then_inc(silu_ready, 1)
            for c in range(NC):
                unit(c, c, first=(c < 2))
            with e.Fori(1, E1 + 1) as x:
                for c in range(NC):
                    unit(c, NC * x + c)

        def moe1_dve(e):
            norm_dve(e, "ln_d", x3, xf)
            e.sem_inc(xf_ready, 1)
            e.wait_ge(moe1_iota, 1)
            dve_link(e, e.tensor_copy(ids1, ids1_int))
            e.wait_ge(logits1_filled, 1)
            dve_link(e, e.tensor_tensor(logits1, psum_b[:, 0:NT * E1].rearrange("p (t e) -> p t e", e=E1),
                                        router1_b.unsqueeze(1).to_broadcast([P, NT, E1]), ALU.add))
            top_two(e, dve_link, logits1, [picks1[:, k, :, :] for k in range(2)], E1, ids1, largest1, second1, spare1, spare1b, index1)
            e.tensor_tensor(share1, second1, largest1, ALU.subtract).then_inc(gap_ready, 1)
            e.wait_ge(gap_exp, 1)
            dve_link(e, e.tensor_scalar(largest1, share1, 1.0, None, ALU.add))
            dve_link(e, e.reciprocal(largest1, largest1))
            dve_link(e, e.tensor_tensor(share1, share1, largest1, ALU.mult))

            def wide_e(v):
                return v.unsqueeze(2).to_broadcast([P, NT, E1])
            dve_link(e, e.tensor_tensor(spare1, picks1[:, 0, :, :], wide_e(largest1), ALU.mult))
            dve_link(e, e.tensor_tensor(spare1b, picks1[:, 1, :, :], wide_e(share1), ALU.mult))
            dve_link(e, e.memset(weight1, 1.0))
            e.tensor_tensor(weight1[:, :, 0:E1], spare1, spare1b, ALU.add).then_inc(weights1_ready, 1)
            e.wait_ge(weights1_ready, 1)

            def product(c, u, first=False):
                e.wait_ge(silu_ready, u + 1)
                if not first:
                    e.wait_ge(down_filled, u - 1)
                e.tensor_tensor(prod[:, c % 2, :, :].rearrange("p k n -> p (k n)"), silu_g[:, c % 2, :],
                                psum_ab[c % 2][:, KH * CW:2 * KH * CW], ALU.mult).then_inc(prod_ready, 1)

            def add(c, x, u):
                e.wait_ge(down_filled, u + 1)
                for k in range(4):
                    t = 4 * c + k
                    i = e.scalar_tensor_tensor(x3[:, t * D:(t + 1) * D], psum_ab[c % 2][:, k * P:(k + 1) * P],
                                               weight1[:, t, bass.ds(x, 1)], x3[:, t * D:(t + 1) * D], ALU.mult, ALU.add)
                i.then_inc(unit_added, 1)

            product(0, 0, first=True)
            for c in range(1, NC):
                product(c, c, first=(c < 2))
                add(c - 1, 0, c - 1)
            with e.Fori(1, E1 + 1) as x:
                product(0, NC * x)
                add(NC - 1, x - 1, NC * x - 1)
                for c in range(1, NC):
                    product(c, NC * x + c)
                    add(c - 1, x, NC * x + c - 1)
            add(NC - 1, E1, UNITS - 1)

        out_stored = sem("out_stored")
        block = ctx.enter_context(nc.Block())

        @block.sync
        def _(e):
            mamba_loads(e)
            moe0_zero(e)
            attention_loads(e)
            att_sync(e, att0)
            moe0_sync(e)
            att_sync(e, att1)
            moe1_sync(e)
            for c in range(NC):
                e.wait_ge(unit_added, UNITS - NC + c + 1)
                e.dma_start(out.rearrange("b (t p) d -> p (b t) d", p=P)[:, 4 * c:4 * c + 4, :],
                            tiled(x3)[:, 4 * c:4 * c + 4, :]).then_inc(out_stored, 16)
            e.wait_ge(out_stored, 16 * NC)
            e.wait_ge(dram_zeroed, ZEROED)

        @block.gpsimd
        def _(e):
            e.memset(zeros[:, :], 0.0).then_inc(zeros_set, 1)
            constants_pool(e)
            mamba_pool(e)
            att0_before_pool(e)
            att_pool(e, att0)
            moe0_pool(e)
            att_pool(e, att1)
            moe1_pool(e)

        @block.scalar
        def _(e):
            mamba_act(e)
            norm_act(e, 'ln_b')
            norm_act(e, 'ln_b1')
            att_act(e, att0)
            moe0_act(e)
            norm_act(e, 'ln_c')
            att_act(e, att1)
            moe1_act(e)

        @block.vector
        def _(e):
            mamba_dve(e)
            att0_before_dve(e)
            att_dve(e, att0, att0_finish)
            moe0_dve(e)
            att1_before_dve(e)
            att_dve(e, att1, att1_finish)
            moe1_dve(e)

        @block.tensor
        def _(e):
            mamba_pe(e)
            att_pe(e, att0)
            moe0_pe(e)
            att_pe(e, att1)
            moe1_pe(e)


_INS = [
    'L0_attn_x', 'L0_attn_W_in_o', 'L0_attn_b_in_o', 'L0_attn_W_out_o', 'L0_attn_b_out_o', 'L0_attn_W_in_i',
    'L0_attn_conv_w', 'L0_attn_conv_b', 'L0_attn_W_xp', 'L0_attn_W_dt', 'L0_attn_b_dt', 'L0_attn_A_log',
    'L0_attn_D_skip', 'L0_attn_W_out_i', 'L0_ffn_ln1_w', 'L0_ffn_ln1_b', 'L0_ffn_q_w', 'L0_ffn_q_b',
    'L0_ffn_k_w', 'L0_ffn_k_b', 'L0_ffn_v_w', 'L0_ffn_v_b', 'L0_ffn_o_w', 'L0_ffn_o_b', 'L0_ffn_ln2_w',
    'L0_ffn_ln2_b', 'L0_ffn_router_w', 'L0_ffn_fc1_w', 'L0_ffn_fc1_b', 'L0_ffn_fc2_w', 'L0_ffn_fc2_b',
    'L1_attn_Wq', 'L1_attn_Wk', 'L1_attn_Wv', 'L1_attn_Wo', 'L1_ffn_router_w', 'L1_ffn_experts_bias',
    'L1_ffn_w1', 'L1_ffn_w3', 'L1_ffn_w2', 'L1_ffn_sw1', 'L1_ffn_sw3', 'L1_ffn_sw2'
]
_OUTS = [((1, 2048, 128), 'float32')]


def kernel(**inputs):
    import numpy as _np
    import concourse.bacc as _bacc
    from concourse import mybir as _mybir
    from concourse.bass_utils import run_bass_kernel_spmd as _run

    nc = _bacc.Bacc("TRN2", target_bir_lowering=False, num_devices=1)
    arrays, args = {}, {}
    for name in _INS:
        v = _np.ascontiguousarray(inputs[name])
        arrays[f"in_{name}_dram"] = v
        args[name] = nc.dram_tensor(f"in_{name}_dram", v.shape, _mybir.dt.from_np(v.dtype), kind="ExternalInput").ap()
    shape, dtype = _OUTS[0]
    out = nc.dram_tensor("out_0_dram", shape, _mybir.dt.from_np(_np.dtype(dtype)), kind="ExternalOutput").ap()
    program(nc, args, out)
    r = _run(nc, [arrays], core_ids=[0])
    return r.results[0]["out_0_dram"]
```

```python
from contextlib import ExitStack

import concourse.bass as bass
from concourse import mybir

ALU = mybir.AluOpType
ACT = mybir.ActivationFunctionType
AX = mybir.AxisListType
F32 = mybir.dt.float32
BF16 = mybir.dt.bfloat16
I32 = mybir.dt.int32

P = 128
T = 2048
D = 128
NT = T // P
CW = 512
NC = T // CW
DI = 256
NM = DI // P
NS = 16
HALF = T // 2
EPS = 1e-5
NEG = -3.0e38
NH = 16
HD = D // NH
SCORE_SCALE = HD ** -0.5
ROWS = 9 * HD
E0, F0, CAP = 16, 512, 2 * (T // 16)
E1, F1 = 8, 256
SLOTS = E0 * CAP


def ds(i, n):
    return bass.ds(i * n, n)


def program(nc, a, out):
    with ExitStack() as ctx:
        ctx.enter_context(nc.allow_non_contiguous_dma(reason="small per-channel vectors"))

        def sb(name, shape, dt=F32):
            return ctx.enter_context(nc.sbuf_tensor(name, shape, dt))

        def sem(name):
            return ctx.enter_context(nc.semaphore(name))

        arena = sb("arena", [P, 18, T])
        extra = sb("extra", [P, 4112])
        psum_a = ctx.enter_context(nc.psum_tensor("psum_a", [P, T], F32))
        psum_b = ctx.enter_context(nc.psum_tensor("psum_b", [P, T], F32))
        psum_ab = [psum_a, psum_b]

        def slot(i):
            return arena[:, i, :]

        def pair(i):
            return arena[:, i:i + 2, :]

        def tiled(ap):
            return ap.rearrange("p (t d) -> p t d", d=D)

        ident = sb("ident", [P, P])
        ident_bf = sb("ident_bf", [P, P], BF16)
        ones_row = sb("ones_row", [1, P])
        ones_bf = sb("ones_bf", [P, P], BF16)
        tri_bf = sb("tri_bf", [P, P], BF16)
        mask_q = sb("mask_q", [P, P], BF16)
        mask_k = sb("mask_k", [P, CW], BF16)
        select = sb("select", [96, 2 * NS, P], BF16)
        sum_groups = sb("sum_groups", [P, 2 * (HD + 1)])
        w_in_o = sb("w_in_o", [P, 2 * DI])
        w_in_i = sb("w_in_i", [P, NM, 2 * DI])
        w_xp = sb("w_xp", [P, NM, P + 2 * NS])
        w_dt = sb("w_dt", [P, DI])
        w_out_i = sb("w_out_i", [P, NM, DI])
        w_out_o = sb("w_out_o", [P, NM, D])
        vec = sb("vec", [P, 64])
        b_in, conv_b, b_dt, d_skip = vec[:, 0:4], vec[:, 4:6], vec[:, 6:8], vec[:, 8:10]
        conv_w = vec[:, 16:24].rearrange("p (m k) -> p m k", m=NM)
        q_b, k_b, q_b_scaled = vec[:, 24:25], vec[:, 25:26], vec[:, 26:27]
        a_neg = sb("a_neg", [P, NM, NS])
        rows = sb("rows", [P, 7, D])
        b_out_row, ln1_w, ln1_b, v_b_row, o_b_row, ln2_w, ln2_b = (rows[:, i, :] for i in range(7))
        w_att = [sb(f"w_att{i}", [P, 4, D]) for i in range(2)]
        w_raw = sb("w_raw", [P, 4, D])
        stats = sb("stats", [P, NT, 6])
        meanvar = sb("meanvar", [P, NT, 2])
        spread = sb("spread", [P, NT])
        carry = sb("carry", [P, NM, NS])

        x_loaded = sem("x_loaded")
        mamba_weights_loaded = sem("mamba_weights_loaded")
        attention_weights_loaded = sem("attention_weights_loaded")
        consts_zeroed = sem("consts_zeroed")
        consts_ready = sem("consts_ready")
        NCONST = 9
        dve_step = sem("dve_step")
        act_step = sem("act_step")
        pool_step = sem("pool_step")
        NORMS = ["ln_a", "ln_b", "ln_b1", "ln_b2", "ln_c", "ln_d"]
        tile_stats, tile_aggr, var_ready, std_ready, rstd_ready, tile_normed = (
            sem(n) for n in ("tile_stats", "tile_aggr", "var_ready", "std_ready", "rstd_ready", "tile_normed"))

        def normed(name):
            return NC * (NORMS.index(name) + 1)

        def turn_normed(e, name, xn, filled):
            for c in range(NC):
                e.wait_ge(tile_normed, normed(name) - NC + c + 1)
                for t in range(4 * c, 4 * c + 4):
                    i = e.transpose(psum_a[:, t * P:(t + 1) * P], xn[:, t * P:(t + 1) * P], ident[:, :])
                i.then_inc(filled, 1)

        def read_turned(e, xT, filled, read):
            for c in range(NC):
                e.wait_ge(filled, c + 1)
                e.activation(xT[:, c * CW:(c + 1) * CW], psum_a[:, c * CW:(c + 1) * CW], ACT.Copy).then_inc(read, 1)

        counts = {"dve": 0, "act": 0, "pool": 0}

        def dve_link(e, ins):
            counts["dve"] += 1
            ins.then_inc(dve_step, 1)
            e.wait_ge(dve_step, counts["dve"])

        def act_link(e, ins):
            counts["act"] += 1
            ins.then_inc(act_step, 1)
            e.wait_ge(act_step, counts["act"])

        def pool_link(e, ins):
            counts["pool"] += 1
            ins.then_inc(pool_step, 1)
            e.wait_ge(pool_step, counts["pool"])

        def norm_dve(e, name, src, dst, affine=None):
            n = NORMS.index(name)
            with e.Fori(0, NC) as c:
                for k in range(4):
                    e.bn_stats(stats[:, bass.ds(4 * c + k, 1), :].rearrange("p a b -> p (a b)"),
                               src[:, ds(4 * c + k, D)]).then_inc(tile_stats, 1)
            e.wait_ge(tile_stats, NT * (n + 1))
            for t in range(NT):
                e.bn_aggr(meanvar[:, t, :], stats[:, t, :]).then_inc(tile_aggr, 1)
            e.wait_ge(tile_aggr, NT * (n + 1))
            e.tensor_scalar(spread[:, :], meanvar[:, :, 1], EPS, None, ALU.add).then_inc(var_ready, 1)
            e.wait_ge(std_ready, n + 1)
            e.reciprocal(spread[:, :], spread[:, :]).then_inc(rstd_ready, 1)
            e.wait_ge(rstd_ready, n + 1)
            for c in range(NC):
                for t in range(4 * c, 4 * c + 4):
                    i = e.tensor_scalar(dst[:, t * D:(t + 1) * D], src[:, t * D:(t + 1) * D], meanvar[:, t:t + 1, 0],
                                        spread[:, t:t + 1], ALU.subtract, ALU.mult)
                if affine is not None:
                    chunk = tiled(dst)[:, 4 * c:4 * c + 4, :]
                    for row, op in zip(affine, (ALU.mult, ALU.add)):
                        dve_link(e, i)
                        i = e.tensor_tensor(chunk, chunk, row.unsqueeze(1).to_broadcast([P, 4, D]), op)
                i.then_inc(tile_normed, 1)
            e.wait_ge(tile_normed, normed(name))

        def norm_act(e, name):
            e.wait_ge(var_ready, NORMS.index(name) + 1)
            e.activation(spread[:, :], spread[:, :], ACT.Sqrt).then_inc(std_ready, 1)

        x_tok = slot(0)
        xn, xT = slot(1), slot(2)
        x_proj = [slot(3), slot(4)]
        gate_out = [slot(5), slot(6)]
        xm = extra[:, 0:2 * 2056].rearrange("p (m n) -> p m n", m=NM)
        conv = [slot(7), slot(8)]
        xc = pair(9)
        gate_in = pair(11)
        dtT = slot(3)
        bc32 = arena[0:32, 4, :]
        bc_parts = arena[0:96, 16, :].bitcast(BF16)[:, 0:T]
        delta = pair(7)
        sp_z, sp_w, sp_l = slot(13), slot(14), slot(15)
        du = pair(13)
        dA = [arena[:, 2 + b, :].rearrange("p (m n) -> p m n", m=NM) for b in range(2)]
        dBu = [arena[:, i, :].rearrange("p (m n) -> p m n", m=NM) for i in (4, 1)]
        c_copy = extra[:, 0:HALF]
        hs = arena[:, 15, :].rearrange("p (m n) -> p m n", m=NM)
        hc = arena[:, 17, :].rearrange("p (m n) -> p m n", m=NM)
        out_i = pair(7)
        x1 = slot(1)

        piece_filled = sem("piece_filled")
        piece_freed = sem("piece_freed")
        x_scaled = sem("x_with_bias")
        xm_padded = sem("xm_padded")
        conv_done = sem("conv_done")
        xc_ready = sem("xc_ready")
        bc_split = sem("bc_split")
        sp_z_ready, sp_w_ready, sp_l_ready, delta_ready = (sem(n) for n in ("sp_z_ready", "sp_w_ready", "sp_l_ready", "delta_ready"))
        du_ready = sem("du_ready")
        a_exp = sem("a_exp")
        a_ready = sem("a_ready")
        b_spread, c_spread = sem("b_spread"), sem("c_spread")
        dA_ready = sem("dA_ready")
        dBu_done = sem("dBu_done")
        scan_done = sem("scan_done")
        hc0_done, hc1_done = sem("hc0_done"), sem("hc1_done")
        c_copied = sem("c_copied")
        y_added = sem("y_added")
        yg_ready = sem("yg_ready")
        x1_ready = sem("x1_ready")

        def mamba_loads(e):
            e.dma_start(tiled(x_tok), a["L0_attn_x"].rearrange("b (t p) d -> p (b t) d", p=P)).then_inc(x_loaded, 16)
            loads = [
                (w_in_o[:, :], a["L0_attn_W_in_o"]),
                (b_in, a["L0_attn_b_in_o"].rearrange("(m p) -> p m", p=P)),
                (w_in_i[:, :, :], a["L0_attn_W_in_i"].rearrange("(k p) n -> p k n", p=P)),
                (conv_w, a["L0_attn_conv_w"].rearrange("(m p) k -> p m k", p=P)),
                (conv_b, a["L0_attn_conv_b"].rearrange("(m p) -> p m", p=P)),
                (w_xp[:, :, :], a["L0_attn_W_xp"].rearrange("(k p) n -> p k n", p=P)),
                (w_dt[:, :], a["L0_attn_W_dt"]),
                (b_dt, a["L0_attn_b_dt"].rearrange("(m p) -> p m", p=P)),
                (a_neg[:, :, :], a["L0_attn_A_log"].rearrange("(m p) n -> p m n", p=P)),
                (d_skip, a["L0_attn_D_skip"].rearrange("(m p) -> p m", p=P)),
                (w_out_i[:, :, :], a["L0_attn_W_out_i"].rearrange("(k p) n -> p k n", p=P)),
                (w_out_o[:, :, :], a["L0_attn_W_out_o"].rearrange("(k p) n -> p k n", p=P)),
                (b_out_row, row_of(a["L0_attn_b_out_o"])),
            ]
            for dst, src in loads:
                e.dma_start(dst, src).then_inc(mamba_weights_loaded, 16)
        MAMBA_LOADS = 13

        def row_of(v):
            return v.rearrange("(a n) -> a n", a=1).to_broadcast([P, v.shape[0]])

        def constants_pool(e):
            for i, (m, v) in enumerate([(ident[:, :], 0.0), (ident_bf[:, :], 0.0), (mask_q[:, :], 0.0),
                                        (tri_bf[:, :], 1.0), (mask_k[:, :], 0.0), (select[:, :, :], 0.0),
                                        (sum_groups[:, :], 0.0), (ones_bf[:, :], 1.0), (ones_row[:, :], 1.0)]):
                e.memset(m, v).then_inc(consts_zeroed, 1)
            e.wait_ge(consts_zeroed, 9)
            for m in (ident, ident_bf):
                e.affine_select(out=m[:, :], in_=m[:, :], compare_op=ALU.not_equal, fill=1.0, base=0,
                                pattern=[[-1, P]], channel_multiplier=1).then_inc(consts_ready, 1)
            e.affine_select(out=mask_q[:, :], in_=mask_q[:, :], compare_op=ALU.is_ge, fill=NEG, base=0,
                            pattern=[[-1, P]], channel_multiplier=1).then_inc(consts_ready, 1)
            e.affine_select(out=tri_bf[:, :], in_=tri_bf[:, :], compare_op=ALU.is_ge, fill=0.0, base=0,
                            pattern=[[1, P]], channel_multiplier=-1).then_inc(consts_ready, 1)
            e.affine_select(out=mask_k[:, :], in_=mask_k[:, :], compare_op=ALU.is_ge, fill=NEG, base=P - CW,
                            pattern=[[1, CW]], channel_multiplier=-1).then_inc(consts_ready, 1)
            for g in range(3):
                e.wait_ge(consts_ready, 5 + g)
                e.affine_select(out=select[32 * g:32 * g + 32, :, :], in_=select[32 * g:32 * g + 32, :, :],
                                compare_op=ALU.not_equal, fill=1.0, base=0,
                                pattern=[[-1, 2 * NS], [0, P]], channel_multiplier=1).then_inc(consts_ready, 1)
            for g in range(4):
                e.wait_ge(consts_ready, 8 + g)
                e.affine_select(out=sum_groups[32 * g:32 * g + 32, :], in_=sum_groups[32 * g:32 * g + 32, :],
                                compare_op=ALU.not_equal, fill=1.0, base=0,
                                pattern=[[-1, 2 * (HD + 1)]], channel_multiplier=1).then_inc(consts_ready, 1)
        CONSTS = 12

        def mamba_pool(e):
            e.wait_ge(consts_ready, CONSTS)
            e.memset(xm[:, :, 0:3], 0.0).then_inc(xm_padded, 1)
            e.wait_ge(mamba_weights_loaded, 16 * MAMBA_LOADS)
            e.wait_ge(tile_normed, normed("ln_a"))
            e.tensor_tensor(tiled(x_tok), tiled(x_tok), b_out_row.unsqueeze(1).to_broadcast([P, NT, D]), ALU.add).then_inc(x_scaled, 1)

            def state(step, first=False):
                e.wait_ge(c_copied, step + 1)
                e.wait_ge(scan_done, 2 * step + 1)
                if not first:
                    e.wait_ge(y_added, 2 * step - 1)
                e.tensor_tensor(hc[:, 0, :], hs[:, 0, :], c_copy, ALU.mult).then_inc(hc0_done, 1)
            state(0, first=True)
            with e.Fori(1, 2 * NS) as step:
                state(step)

        def mamba_pe(e):
            e.wait_ge(consts_ready, CONSTS)
            e.wait_ge(mamba_weights_loaded, 16 * MAMBA_LOADS)

            def piece(n, emit, free=None):
                if n >= 2:
                    e.wait_ge(piece_freed, n - 1)
                emit(psum_ab[n % 2]).then_inc(piece_filled, 1)

            def transposes(ps):
                for t in range(NT):
                    i = e.transpose(ps[:, t * P:(t + 1) * P], xn[:, t * P:(t + 1) * P], ident[:, :])
                return i

            def product(lhs, rhs, m=P):
                def emit(ps):
                    for c in range(NC):
                        for k in range(len(lhs)):
                            i = e.matmul(ps[0:m, c * CW:(c + 1) * CW], lhs[k], rhs[k][:, c * CW:(c + 1) * CW],
                                         start=(k == 0), stop=(k == len(lhs) - 1))
                    return i
                return emit

            e.wait_ge(tile_normed, normed("ln_a"))
            piece(0, transposes)
            e.wait_ge(piece_freed, 1)
            for m in range(4):
                piece(1 + m, product([w_in_o[:, m * P:(m + 1) * P]], [xT]))
            e.wait_ge(piece_freed, 3)
            for m in range(4):
                piece(5 + m, product([w_in_i[:, k, m * P:(m + 1) * P] for k in range(NM)], x_proj))
            e.wait_ge(xc_ready, NM)
            piece(9, product([w_xp[:, k, 0:P] for k in range(NM)], [xc[:, k, :] for k in range(NM)]))
            piece(10, product([w_xp[:, k, P:P + 2 * NS] for k in range(NM)], [xc[:, k, :] for k in range(NM)], 2 * NS))
            e.wait_ge(piece_freed, 10)
            for m in range(NM):
                piece(11 + m, product([w_dt[:, m * P:(m + 1) * P]], [dtT]))
            e.wait_ge(piece_freed, 13)
            e.wait_ge(bc_split, 1)

            for h in range(2):
                if h:
                    e.wait_ge(yg_ready, h)
                cols = slice(h * HALF, (h + 1) * HALF)

                def spread_row(r, dst, done):
                    for c in range(2):
                        i = e.matmul(dst[:, c * CW:(c + 1) * CW], select[:, bass.ds(r, 1), :].rearrange("p a b -> p (a b)"),
                                     bc_parts[:, h * HALF + c * CW:h * HALF + (c + 1) * CW], start=True, stop=True)
                    i.then_inc(done, 1)

                def add_y(m, step, start, stop):
                    e.wait_ge((hc0_done, hc1_done)[m], step + 1)
                    for c in range(2):
                        i = e.matmul(psum_b[:, m * HALF + c * CW:m * HALF + (c + 1) * CW], ident[:, :],
                                     hc[:, m, c * CW:(c + 1) * CW], start=start, stop=stop, skip_group_check=True)
                    i.then_inc(y_added, 1)

                if h:
                    e.wait_ge(dBu_done, NS * h)
                spread_row(0, psum_a[:, 0:HALF], b_spread)
                if h:
                    e.wait_ge(hc1_done, NS * h)
                    e.wait_ge(c_copied, NS * h)
                spread_row(NS, psum_a[:, HALF:T], c_spread)

                def state(n, first=False, ahead=True):
                    step = h * NS + n
                    e.wait_ge(hc1_done, step + 1)
                    e.wait_ge(c_copied, step + 1)
                    spread_row(NS + n + 1, psum_a[:, HALF:T], c_spread)
                    if ahead:
                        e.wait_ge(dBu_done, step + 2)
                        spread_row(n + 2, psum_a[:, 0:HALF], b_spread)
                    for m in range(NM):
                        add_y(m, step, first, False)

                e.wait_ge(dBu_done, h * NS + 1)
                spread_row(1, psum_a[:, 0:HALF], b_spread)
                state(0, first=True)
                with e.Fori(1, NS - 2) as n:
                    state(n)
                state(NS - 2, ahead=False)
                for m in range(NM):
                    add_y(m, h * NS + NS - 1, False, True)

            def out_tokens(ps):
                for t in range(NT):
                    for k in range(NM):
                        i = e.matmul(ps[:, t * P:(t + 1) * P], out_i[:, k, t * P:(t + 1) * P], w_out_o[:, k, :],
                                     start=(k == 0), stop=(k == NM - 1))
                return i

            e.wait_ge(yg_ready, 2)
            for m in range(NM):
                piece(13 + m, product([w_out_i[:, k, m * P:(m + 1) * P] for k in range(NM)], [gate_in[:, k, :] for k in range(NM)]))
            e.wait_ge(piece_freed, 15)
            piece(15, out_tokens)

        def mamba_act(e):
            e.wait_ge(mamba_weights_loaded, 16 * MAMBA_LOADS)
            norm_act(e, "ln_a")
            e.activation(a_neg[:, :, :], a_neg[:, :, :], ACT.Exp).then_inc(a_exp, 1)

            def read(n, dst, func, bias=None, m=P):
                e.wait_ge(piece_filled, n + 1)
                if bias is None:
                    e.activation(dst, psum_ab[n % 2][0:m, :], func).then_inc(piece_freed, 1)
                else:
                    e.activation(dst, psum_ab[n % 2][0:m, :], func, bias=bias).then_inc(piece_freed, 1)

            read(0, xT, ACT.Copy)
            for m in range(NM):
                read(1 + m, x_proj[m], ACT.Identity, b_in[:, m:m + 1])
            for m in range(NM):
                read(3 + m, gate_out[m], ACT.Sigmoid, b_in[:, 2 + m:3 + m])
            for m in range(NM):
                read(5 + m, xm[:, m, 3:3 + T], ACT.Copy)
            for m in range(NM):
                read(7 + m, gate_in[:, m, :], ACT.Silu)
            for m in range(NM):
                e.wait_ge(conv_done, m + 1)
                e.activation(xc[:, m, :], conv[m], ACT.Silu).then_inc(xc_ready, 1)
            read(9, dtT, ACT.Copy)
            read(10, bc32, ACT.Copy, m=32)
            for m in range(NM):
                read(11 + m, delta[:, m, :], ACT.Identity, b_dt[:, m:m + 1])
            e.wait_ge(piece_freed, 13)
            for m in range(NM):
                if m:
                    e.wait_ge(delta_ready, m)
                act_link(e, e.activation(sp_z, delta[:, m, :], ACT.Abs))
                e.activation(sp_z, sp_z, ACT.Exp, scale=-1.0).then_inc(sp_z_ready, 1)
                e.wait_ge(sp_w_ready, m + 1)
                e.activation(sp_l, sp_w, ACT.Ln).then_inc(sp_l_ready, 1)
            e.wait_ge(delta_ready, NM)
            e.wait_ge(a_ready, 1)

            def decay(h, n, b, first=False):
                if not first:
                    e.wait_ge(scan_done, 2 * (h * NS + n) - 2)
                for m in range(NM):
                    e.activation(dA[b][:, m, :], delta[:, m, h * HALF:(h + 1) * HALF], ACT.Exp,
                                 scale=a_neg[:, m, bass.ds(n, 1)]).then_inc(dA_ready, 1)
            def copy_c(step, first=False):
                e.wait_ge(c_spread, step + 1)
                if not first:
                    e.wait_ge(hc0_done, step)
                e.activation(c_copy, psum_a[:, HALF:T], ACT.Copy).then_inc(c_copied, 1)

            for h in range(2):
                decay(h, 0, 0, first=(h == 0))
                copy_c(h * NS, first=(h == 0))
                decay(h, 1, 1, first=(h == 0))
                with e.Fori(1, NS // 2) as i:
                    copy_c(h * NS + 2 * i - 1)
                    decay(h, 2 * i, 0)
                    copy_c(h * NS + 2 * i)
                    decay(h, 2 * i + 1, 1)
                copy_c(h * NS + NS - 1)

        def mamba_dve(e):
            e.wait_ge(x_loaded, 16)
            norm_dve(e, "ln_a", x_tok, xn)
            e.wait_ge(a_exp, 1)
            e.tensor_scalar(a_neg[:, :, :], a_neg[:, :, :], -1.0, None, ALU.mult).then_inc(a_ready, 1)
            e.wait_ge(xm_padded, 1)
            e.wait_ge(mamba_weights_loaded, 16 * MAMBA_LOADS)
            for m in range(NM):
                e.wait_ge(piece_freed, 6 + m)
                dve_link(e, e.tensor_scalar(conv[m], xm[:, m, 0:T], conv_w[:, m, 0:1], conv_b[:, m:m + 1], ALU.mult, ALU.add))
                for k in range(1, 4):
                    i = e.scalar_tensor_tensor(conv[m], xm[:, m, k:k + T], conv_w[:, m, k:k + 1], conv[m], ALU.mult, ALU.add)
                    if k < 3:
                        dve_link(e, i)
                    else:
                        i.then_inc(conv_done, 1)
            e.wait_ge(piece_freed, 11)
            rest = arena[0:32, 17, :]
            dve_link(e, e.tensor_copy(bc_parts[0:32, :], bc32))
            dve_link(e, e.tensor_tensor(rest, bc32, bc_parts[0:32, :], ALU.subtract))
            dve_link(e, e.tensor_copy(bc_parts[32:64, :], rest))
            dve_link(e, e.tensor_copy(arena[0:32, 16, 1024:2048].bitcast(BF16), rest))
            dve_link(e, e.tensor_tensor(rest, rest, arena[0:32, 16, 1024:2048].bitcast(BF16), ALU.subtract))
            e.tensor_copy(bc_parts[64:96, :], rest).then_inc(bc_split, 1)
            e.wait_ge(piece_freed, 13)
            for m in range(NM):
                e.wait_ge(sp_z_ready, m + 1)
                e.tensor_scalar(sp_w, sp_z, 1.0, None, ALU.add).then_inc(sp_w_ready, 1)
                e.wait_ge(sp_l_ready, m + 1)
                dve_link(e, e.scalar_tensor_tensor(sp_z, sp_w, -1.0, sp_z, ALU.add, ALU.subtract))
                dve_link(e, e.scalar_tensor_tensor(sp_l, delta[:, m, :], 0.0, sp_l, ALU.max, ALU.add))
                e.tensor_tensor(delta[:, m, :], sp_l, sp_z, ALU.subtract).then_inc(delta_ready, 1)
                e.wait_ge(delta_ready, m + 1)
            e.tensor_tensor(du, delta, xc, ALU.mult).then_inc(du_ready, 1)
            e.wait_ge(du_ready, 1)

            for h in range(2):
                cols = slice(h * HALF, (h + 1) * HALF)

                def weighted_input(n, b):
                    e.wait_ge(b_spread, h * NS + n + 1)
                    e.tensor_tensor(dBu[b], du[:, :, cols], psum_a[:, 0:HALF].unsqueeze(1).to_broadcast([P, NM, HALF]),
                                    ALU.mult).then_inc(dBu_done, 1)

                def state(n, b, first=False, last=False):
                    step = h * NS + n
                    e.wait_ge(dBu_done, step + 1)
                    if not first:
                        e.wait_ge(hc0_done, step)
                        e.wait_ge(hc1_done, step)
                    for m in range(NM):
                        e.wait_ge(dA_ready, 2 * step + m + 1)
                        start = 0.0 if h == 0 else carry[:, m, bass.ds(n, 1)]
                        e.tensor_tensor_scan(hs[:, m, :], dA[b][:, m, :], dBu[b][:, m, :], start, ALU.mult, ALU.add).then_inc(scan_done, 1)
                    if not last:
                        weighted_input(n + 1, 1 - b)
                    e.wait_ge(scan_done, 2 * step + 2)
                    if h == 0:
                        e.tensor_copy(carry[:, :, bass.ds(n, 1)], hs[:, :, HALF - 1:HALF])
                    e.wait_ge(c_copied, step + 1)
                    if not first:
                        e.wait_ge(y_added, 2 * step)
                    e.tensor_tensor(hc[:, 1, :], hs[:, 1, :], psum_a[:, HALF:T], ALU.mult).then_inc(hc1_done, 1)

                weighted_input(0, 0)
                state(0, 0, first=(h == 0))
                state(1, 1)
                with e.Fori(1, NS // 2 - 1) as i:
                    state(2 * i, 0)
                    state(2 * i + 1, 1)
                state(NS - 2, 0)
                state(NS - 1, 1, last=True)
                e.wait_ge(y_added, (h + 1) * 2 * NS)
                for m in range(NM):
                    i = e.scalar_tensor_tensor(hs[:, m, :], xc[:, m, cols], d_skip[:, m:m + 1],
                                               psum_b[:, m * HALF:(m + 1) * HALF], ALU.mult, ALU.add)
                    dve_link(e, i)
                e.tensor_tensor(gate_in[:, :, cols], hs, gate_in[:, :, cols], ALU.mult).then_inc(yg_ready, 1)
                e.wait_ge(yg_ready, h + 1)
            for m in range(NM):
                e.wait_ge(piece_filled, 14 + m)
                e.tensor_tensor(out_i[:, m, :], psum_ab[(13 + m) % 2][:, :], gate_out[m], ALU.mult).then_inc(piece_freed, 1)
            e.wait_ge(piece_filled, 16)
            e.wait_ge(x_scaled, 1)
            e.tensor_tensor(x1, psum_ab[15 % 2][:, :], x_tok, ALU.add).then_inc(x1_ready, 1)
            e.wait_ge(x1_ready, 1)
        QT = NT
        GROUPS = []
        for c in range(NC):
            for j in range(0, 4 * c, 2):
                GROUPS.append((c, [(j, CW, 0, 0), (j + 1, CW, CW, 0)]))
            if c == 0:
                GROUPS += [(0, [(0, CW, 0, P), (1, CW, CW, 2 * P)]), (0, [(2, CW, 0, 3 * P), (3, CW, CW, 4 * P)])]
            else:
                GROUPS += [(c, [(4 * c, 4 * P, 0, P), (4 * c + 1, 3 * P, CW, P)]),
                           (c, [(4 * c + 2, 2 * P, 0, P), (4 * c + 3, P, 2 * P, P)])]
        NG = len(GROUPS)
        NP = NG // 2
        LAST = [max(g for g in range(NG) if GROUPS[g][0] == c) for c in range(NC)]
        FIRST = [min(g for g in range(NG) if GROUPS[g][0] == c) for c in range(NC)]
        MAX_PIECES = [[(0, 0, P, 0), (1, 0, 2 * P, P)]]
        MAX_PIECES += [[(i, c, min(CW, (i + 1) * P - c * CW), 0)] for i in range(2, QT) for c in range(i // 4 + 1)]
        NB = 3

        AHEAD_MAX = 18

        def step_order(turns, maxima=True, early=True, scores=True):
            def vector_time(x):
                if x[0] == "max":
                    return sum(60 + b[2] for b in MAX_PIECES[x[1]]) + (900 if x[1] == len(MAX_PIECES) - 1 else 0)
                return 200
            order = []
            queue = [("max", n, 1) for n in range(AHEAD_MAX, len(MAX_PIECES))] if maxima else []
            found = len(queue)
            queue += [("max", n, 2) for n in range(AHEAD_MAX)] if early else []
            if maxima:
                queue.insert(min(found + 3, len(queue)), ("maxrow", 0, 1))
            total = sum(vector_time(x) for x in queue) + (NC * 600 if turns else 0)
            done = 0
            for t in range(NG):
                g = t + 2
                if g < NG or scores:
                    order.append(("scores", g % NG, g // NG))
                while len(queue) > (2 if early else 0) and done < total * (t + 1) / (NG if early else 3 * NG // 5):
                    done += vector_time(queue[0])
                    order.append(queue.pop(0))
                if t % 2:
                    order.append(("context", t // 2, 0))
                    if turns and t in LAST:
                        done += 600
                    for c in range(NC - 1):
                        if turns and t // 2 == LAST[c] // 2 + 1:
                            order.append(("turn", c, 0))
            return order + queue + ([("turn", NC - 1, 0)] if turns else [])

        def ring_of(order):
            return [x for x in order if x[0] in ("max", "maxrow", "turn")]

        ORDERS = [step_order(turns=False), step_order(turns=True)]
        RINGS = [ring_of(order) for order in ORDERS]
        PAIR = sum(len(ring) for ring in RINGS)
        assert PAIR % NB == 0
        PAIRS = NH // 2
        LAST_ORDERS = [step_order(turns=False, early=False), step_order(turns=True, maxima=False, early=False, scores=False)]
        LAST_RINGS = [ring_of(order) for order in LAST_ORDERS]
        FIRST_RING = ([("max", n, 1) for n in range(len(MAX_PIECES))] + [("max", n, 2) for n in range(3)] + [("maxrow", 0, 1)]
                      + [("max", n, 2) for n in range(3, AHEAD_MAX)])
        AHEAD = NB + -len(FIRST_RING) % NB
        START = AHEAD + len(FIRST_RING)

        def is_last(pair):
            return isinstance(pair, int) and pair == PAIRS - 1

        def order_of(pair, b):
            return (LAST_ORDERS if is_last(pair) else ORDERS)[b]

        def rings_of(pair):
            return LAST_RINGS if is_last(pair) else RINGS

        def first_piece(pair, b):
            return START + pair * PAIR + b * len(rings_of(pair)[0])

        def phase(pair, b):
            return (START + b * len(rings_of(pair)[0])) % NB

        def turned(pair, c):
            return first_piece(pair, 1) + rings_of(pair)[1].index(("turn", c, 0)) + 1

        class Attention:
            pass

        def attention(L, x_in, norm, w_cols, wt_raw):
            s = Attention()
            s.xT_filled = sem(f"att{L}_xT_filled")
            s.xT_read = sem(f"att{L}_xT_read")
            s.qkv_filled = sem(f"att{L}_qkv_filled")
            s.qkv_read = sem(f"att{L}_qkv_read")
            s.qk_split = sem(f"att{L}_qk_split")
            s.parts_stored = sem(f"att{L}_parts_stored")
            s.ring_filled = sem(f"att{L}_ring_filled")
            s.ring_freed = sem(f"att{L}_ring_freed")
            s.scores_filled = sem(f"att{L}_scores_filled")
            s.exp_done = sem(f"att{L}_exp_done")
            s.context_done = sem(f"att{L}_context_done")
            s.context_read = sem(f"att{L}_context_read")
            s.maxrow_split = sem(f"att{L}_maxrow_split")
            s.maxrow_turned = sem(f"att{L}_maxrow_turned")
            s.value_staged = sem(f"att{L}_value_staged")
            s.staging_set = sem(f"att{L}_staging_set")
            s.weights_turned = sem(f"att{L}_weights_turned")
            s.weights_read = sem(f"att{L}_weights_read")
            s.ctx_turned = sem(f"att{L}_ctx_turned")
            s.ctx_read = sem(f"att{L}_ctx_read")
            s.out_filled = sem(f"att{L}_out_filled")
            s.ones_set = sem(f"att{L}_ones_set")
            s.split_step = sem(f"att{L}_split_step")
            s.recip_ready = sem(f"att{L}_recip_ready")
            s.maxrow_stored = sem(f"att{L}_maxrow_stored")
            s.m_loaded = [sem(f"att{L}_m_loaded{b}") for b in range(2)]
            s.e_loaded = [sem(f"att{L}_e_loaded{b}") for b in range(2)]
            s.maxrow_loaded = [sem(f"att{L}_maxrow_loaded{b}") for b in range(2)]
            s.q_dram = nc.dram_tensor(f"q_parts{L}", [NH, 3, HD, T], BF16).ap()
            s.k_dram = nc.dram_tensor(f"k_parts{L}", [NH, 5, HD, T], BF16).ap()
            s.m_dram = nc.dram_tensor(f"max_rows{L}", [2, 3 * QT, P], BF16).ap()
            s.xn, s.xT = x_in, slot(3)
            s.q_parts = arena[:, 4:6, :].rearrange("p a n -> p (a n)").bitcast(BF16).rearrange("p (i n) -> p i n", i=4)
            s.k_parts = arena[:, 6:8, :].rearrange("p a n -> p (a n)").bitcast(BF16).rearrange("p (i n) -> p i n", i=4)
            s.full, s.rest = [slot(8), slot(16)], slot(9)
            s.v = slot(10)
            s.ctx, s.ctxT = slot(11), slot(3)
            s.mq, s.mk, s.eq, s.ek = (slot(12 + i).bitcast(BF16).rearrange("p (b n) -> p b n", b=2) for i in range(4))
            s.pt = pair(16).rearrange("p a n -> p (a n)").rearrange("p (b n) -> p b n", b=4)
            s.vs = extra[:, 0:1024].rearrange("p (b t c) -> p b t c", b=2, c=32)
            s.oe = slot(9).rearrange("p (c n) -> p c n", c=NC)
            s.mpart = extra[:, 2048:2112].rearrange("p (t c) -> p t c", c=4)
            s.mneg = extra[:, 2112:2128]
            s.mrest = extra[:, 2128:2144]
            s.mparts = extra[:, 2320:2384].bitcast(BF16)
            s.mrow = extra[0:48, 2176:2304].bitcast(BF16).rearrange("p (b n) -> p b n", b=2)
            s.recip = extra[:, 2304:2320].rearrange("p (b t k) -> p b t k", b=2, k=2)
            s.w = w_cols
            s.wt_raw = wt_raw
            s.L = L
            s.norm = norm
            return s

        def ring(n):
            return psum_b[:, (n % NB) * CW:(n % NB + 1) * CW]
        context_bank = psum_b[:, NB * CW:(NB + 1) * CW]

        def ones_column(b):
            return b * (HD + 1) + HD

        def att_sync(e, s):
            e.wait_ge(s.qk_split, 1)
            for i in range(3):
                e.dma_start(s.q_dram[:, i, :, :],
                            s.q_parts[:, i, :]).then_inc(s.parts_stored, 16)
            e.wait_ge(s.qk_split, 2)
            for i in range(5):
                e.dma_start(s.k_dram[:, i, :, :], s.k_parts[:, i % 3, :]).then_inc(s.parts_stored, 16)
            e.wait_ge(s.parts_stored, 8 * 16)
            e.wait_ge(s.ones_set, 1)

            def load(q, k, h, b, done):
                for r in range(3):
                    e.dma_start(q[24 * r:24 * r + 24, b, :],
                                s.q_dram[bass.ds(h, 1), :, :, :].rearrange("a i d t -> (a i d) t")).then_inc(done, 16)
                    e.dma_start(k[24 * r:24 * r + 24, b, :],
                                s.k_dram[bass.ds(h, 1), r:r + 3, :, :].rearrange("a i d t -> (a i d) t")).then_inc(done, 16)

            def maxrow(h, b):
                e.wait_ge(s.maxrow_turned, h + 1)
                e.dma_start(s.m_dram[b, :, :], s.mrow[:, b, :]).then_inc(s.maxrow_stored, 16)
                e.wait_ge(s.maxrow_stored, 16 * (h + 1))
                e.dma_start(s.eq[ROWS:ROWS + 3, b, :], s.m_dram[b, :, :].rearrange("(i t) p -> i (t p)", i=3)).then_inc(s.maxrow_loaded[b], 16)

            def step(h, b, load_max=True):
                e.wait_ge(s.context_done, NP * h + 2)
                load(s.eq, s.ek, h + 1, 1 - b, s.e_loaded[1 - b])
                maxrow(h + 1, 1 - b)
                if load_max:
                    load(s.mq, s.mk, h + 3, 1 - b, s.m_loaded[1 - b])

            load(s.mq, s.mk, 0, 0, s.m_loaded[0])
            load(s.mq, s.mk, 1, 1, s.m_loaded[1])
            load(s.eq, s.ek, 0, 0, s.e_loaded[0])
            maxrow(0, 0)
            load(s.mq, s.mk, 2, 0, s.m_loaded[0])
            with e.Fori(0, NH // 2 - 2) as i:
                step(2 * i, 0)
                step(2 * i + 1, 1)
            for h in range(NH - 4, NH - 1):
                step(h, h % 2, load_max=h + 3 < NH)

        def att_pool(e, s):
            e.wait_ge(s.xT_read, NC)
            e.memset(s.ek[64:ROWS + 3, :, :], 1.0).then_inc(s.ones_set, 1)
            e.wait_ge(s.ones_set, 1)
            e.memset(s.vs[:, :, :, :], 0.0).then_inc(s.staging_set, 1)
            e.wait_ge(s.staging_set, 1)
            for b in range(2):
                e.memset(s.vs[:, b, :, ones_column(b):ones_column(b) + 1], 1.0).then_inc(s.staging_set, 1)
            e.wait_ge(s.qkv_read, 3)

            def stage(h, b):
                e.tensor_copy(s.vs[:, b, :, ones_column(b) - HD:ones_column(b)], tiled(s.v)[:, :, bass.ds(h * HD, HD)]).then_inc(s.value_staged, 1)

            def later(h, b):
                e.wait_ge(s.context_done, NP * (h - 1) + 2)
                stage(h, b)
            stage(0, 0)
            stage(1, 1)
            with e.Fori(1, NH // 2) as i:
                later(2 * i, 0)
                later(2 * i + 1, 1)

        def att_pe(e, s):
            if s.wt_raw is not None:
                e.wait_ge(tile_normed, normed(s.norm) - NC + 1)
                for i in range(4):
                    t = e.transpose(psum_b[:, i * P:(i + 1) * P], s.wt_raw[:, i, :], ident[:, :])
                t.then_inc(s.weights_turned, 1)
                e.wait_ge(s.weights_read, 1)
            turn_normed(e, s.norm, s.xn, s.xT_filled)
            for n in range(2):
                for c in range(NC):
                    if n == 0:
                        e.wait_ge(s.xT_read, c + 1)
                    i = e.matmul(psum_ab[1 - n][:, c * CW:(c + 1) * CW], s.w[:, n, :], s.xT[:, c * CW:(c + 1) * CW], start=True, stop=True)
                i.then_inc(s.qkv_filled, 1)
            e.wait_ge(s.qkv_read, 1)
            for t in range(NT):
                i = e.matmul(psum_b[:, t * P:(t + 1) * P], s.xT[:, t * P:(t + 1) * P], s.w[:, 2, :], start=True, stop=True)
            i.then_inc(s.qkv_filled, 1)
            e.wait_ge(s.qkv_read, 3)
            e.sem_inc(s.ring_filled, AHEAD)
            e.sem_inc(s.context_done, 2)

            def ring_wait(at):
                e.wait_ge(s.ring_freed, at - NB + 1)

            def ring_piece(h, b, n, x):
                ps, kind, k = ring(n), x[0], x[1]
                if kind == "max":
                    for i, c, width, at in MAX_PIECES[k]:
                        diagonal = c == i // 4
                        m = e.matmul(ps[:, at:at + width], s.mq[0:ROWS, b, i * P:(i + 1) * P], s.mk[0:ROWS, b, c * CW:c * CW + width],
                                     start=True, stop=not diagonal)
                        if diagonal:
                            m = e.matmul(ps[:, at + width - P:at + width], ident_bf[:, :], mask_q[:, :], start=False, stop=True)
                else:
                    e.wait_ge(s.maxrow_split, h + 1)
                    m = e.transpose(ps[:, 0:64].bitcast(BF16), s.mparts[:, :], ident_bf[:, :])
                m.then_inc(s.ring_filled, 1)


            def scores_group(h, b, g):
                c, blocks = GROUPS[g]
                e.wait_ge(s.exp_done, NG * h + g + 1)
                for j, width, at, masked in blocks:
                    ps = psum_a[:, (g % 2) * HALF + at:(g % 2) * HALF + at + width]
                    m = e.matmul(ps, s.ek[0:ROWS + 3, b, j * P:(j + 1) * P], s.eq[0:ROWS + 3, b, (c + 1) * CW - width:(c + 1) * CW],
                                 start=True, stop=not masked)
                    if masked:
                        m = e.matmul(ps[:, 0:masked], ident_bf[:, :], mask_k[:, CW - masked:CW], start=False, stop=True)
                m.then_inc(s.scores_filled, 1)

            def context(h, b, p):
                c = GROUPS[2 * p][0]
                e.wait_ge(s.exp_done, NG * h + 2 * p + 4)
                if 2 * p == FIRST[c]:
                    e.wait_ge(s.context_read, NC * h + c + 1)
                for g in (2 * p, 2 * p + 1):
                    for j, width, at, masked in GROUPS[g][1]:
                        k = j % 4
                        m = e.matmul(context_bank[32 * k:32 * k + 32, CW - width:CW], s.vs[:, b, j, :], s.pt[:, g % 4, at:at + width],
                                     start=(j < 4), stop=(j >= 4 * c), skip_group_check=True)
                m.then_inc(s.context_done, 1)

            def turn(pair, c, n):
                e.wait_ge(s.context_read, NC * (2 * pair + 1) + c + 2)
                for t in range(4):
                    m = e.matmul(ring(n)[:, 32 * t:32 * t + 2 * (HD + 1)], s.oe[:, c, t * P:(t + 1) * P], sum_groups[:, :],
                                 start=True, stop=True)
                m.then_inc(s.ring_filled, 1)

            def step(pair, b):
                h, idx = 2 * pair + b, 0
                for kind, k, ahead in order_of(pair, b):
                    if kind == "scores":
                        if ahead and k == 0:
                            e.wait_ge(s.e_loaded[1 - b], 96 * (pair + b + 1))
                            e.wait_ge(s.maxrow_loaded[1 - b], 16 * (pair + b + 1))
                        scores_group(h + ahead, (b + ahead) % 2, k)
                    elif kind == "context":
                        if k == 0:
                            e.wait_ge(s.value_staged, h + 1)
                        context(h, b, k)
                    else:
                        if kind == "max" and ahead == 2 and k == 0:
                            e.wait_ge(s.m_loaded[b], 96 * (pair + 2))
                        ring_wait(first_piece(pair, b) + idx)
                        if kind == "turn":
                            turn(pair, k, phase(pair, b) + idx)
                        else:
                            ring_piece(h + ahead, (b + ahead) % 2, phase(pair, b) + idx, (kind, k))
                        idx += 1

            e.wait_ge(s.m_loaded[0], 96)
            for n, (kind, k, ahead) in enumerate(FIRST_RING):
                if (kind, k, ahead) == ("max", 0, 2):
                    e.wait_ge(s.m_loaded[1], 96)
                ring_wait(AHEAD + n)
                ring_piece(ahead - 1, ahead - 1, AHEAD + n, (kind, k))
            e.wait_ge(s.e_loaded[0], 96)
            e.wait_ge(s.maxrow_loaded[0], 16)
            scores_group(0, 0, 0)
            scores_group(0, 0, 1)
            with e.Fori(0, PAIRS - 1) as i:
                step(i, 0)
                step(i, 1)
            step(PAIRS - 1, 0)
            step(PAIRS - 1, 1)

            e.wait_ge(s.ring_freed, turned(PAIRS - 1, NC - 1))
            for t in range(NT):
                i = e.transpose(psum_a[:, t * P:(t + 1) * P], s.ctx[:, t * P:(t + 1) * P], ident[:, :])
            i.then_inc(s.ctx_turned, 1)
            e.wait_ge(s.ctx_read, 1)
            for t in range(NT):
                i = e.matmul(psum_b[:, t * P:(t + 1) * P], s.ctxT[:, t * P:(t + 1) * P], s.w[:, 3, :], start=True, stop=True)
            i.then_inc(s.out_filled, 1)

        def att_act(e, s):
            if s.wt_raw is not None:
                e.wait_ge(s.weights_turned, 1)
                e.activation(s.w[:, :, :].rearrange("p a n -> p (a n)"), psum_b[:, 0:4 * P], ACT.Copy).then_inc(s.weights_read, 1)
            read_turned(e, s.xT, s.xT_filled, s.xT_read)
            for n, (scale, bias) in enumerate(((SCORE_SCALE, q_b_scaled), (1.0, k_b))):
                e.wait_ge(s.qkv_filled, n + 1)
                if s.L == 0:
                    e.activation(s.full[n], psum_ab[1 - n][:, :], ACT.Identity, scale=scale, bias=bias).then_inc(s.qkv_read, 1)
                else:
                    e.activation(s.full[n], psum_ab[1 - n][:, :], ACT.Copy, scale=scale).then_inc(s.qkv_read, 1)
            if s.L == 1:
                e.wait_ge(s.qkv_filled, 3)
                e.activation(s.v, psum_b[:, :], ACT.Copy).then_inc(s.qkv_read, 1)
            e.wait_ge(s.qkv_read, 3)
            e.sem_inc(s.exp_done, 2)
            e.sem_inc(s.context_read, 1)

            def read_context(pair, c):
                e.wait_ge(s.context_done, NP * (2 * pair) + LAST[c] // 2 + 3)
                e.wait_ge(s.ring_filled, turned(pair - 1, c))
                e.activation(s.oe[:, c, :], context_bank, ACT.Copy).then_inc(s.context_read, 1)

            def exp_group(h, g):
                width = sum(w for _, w, _, _ in GROUPS[g][1])
                e.wait_ge(s.scores_filled, NG * h + g + 1)
                e.wait_ge(s.context_done, NP * h + g // 2 + 1)
                e.activation(s.pt[:, g % 4, 0:width], psum_a[:, (g % 2) * HALF:(g % 2) * HALF + width], ACT.Exp).then_inc(s.exp_done, 1)

            def step(pair, b, last=False):
                for g in range(2, NG + 2):
                    if g < NG or not last:
                        exp_group(2 * pair + b + g // NG, g % NG)
                    if b == 0 and g - 2 in LAST:
                        read_context(pair, LAST.index(g - 2))

            exp_group(0, 0)
            exp_group(0, 1)
            with e.Fori(0, PAIRS - 1) as i:
                step(i, 0)
                step(i, 1)
            step(PAIRS - 1, 0)
            step(PAIRS - 1, 1, last=True)
            e.wait_ge(s.ctx_turned, 1)
            e.activation(s.ctxT, psum_a[:, :], ACT.Copy).then_inc(s.ctx_read, 1)

        def att_dve(e, s, finish):
            for n, parts in enumerate((s.q_parts, s.k_parts)):
                e.wait_ge(s.qkv_read, n + 1)
                dve_link(e, e.tensor_copy(parts[:, 0, :], s.full[n]))
                dve_link(e, e.tensor_tensor(s.rest, s.full[n], parts[:, 0, :], ALU.subtract))
                dve_link(e, e.tensor_copy(parts[:, 1, :], s.rest))
                e.tensor_tensor(parts[:, 2, :], s.rest, parts[:, 1, :], ALU.subtract).then_inc(s.qk_split, 1)
                e.wait_ge(s.qk_split, n + 1)
            if s.L == 0:
                e.wait_ge(s.qkv_filled, 3)
                e.tensor_tensor(tiled(s.v), tiled(psum_b[:, :]), v_b_row.unsqueeze(1).to_broadcast([P, NT, D]), ALU.add).then_inc(s.qkv_read, 1)
            e.wait_ge(s.qkv_read, 3)
            dve_link(e, e.memset(s.mpart, NEG))
            dve_link(e, e.memset(s.mparts, 0.0))
            e.sem_inc(s.ring_freed, AHEAD)

            def link(h, k, ins):
                ins.then_inc(s.split_step, 1)
                e.wait_ge(s.split_step, 4 * h + k + 1)

            def ring_read(pair, b, ps, number, x):
                h = 2 * pair + b + x[2]
                e.wait_ge(s.ring_filled, number + 1)
                if x[0] == "max":
                    for i, c, width, at in MAX_PIECES[x[1]]:
                        m = e.tensor_reduce(s.mpart[:, i, c:c + 1], ps[:, at:at + width], AX.X, ALU.max)
                    m.then_inc(s.ring_freed, 1)
                    if x[1] == len(MAX_PIECES) - 1:
                        e.wait_ge(s.ring_freed, number + 1)
                        link(h, 0, e.tensor_reduce(s.mneg, s.mpart, AX.X, ALU.max, negate=True))
                        link(h, 1, e.tensor_copy(s.mparts[:, 0:16], s.mneg))
                        link(h, 2, e.tensor_tensor(s.mrest, s.mneg, s.mparts[:, 0:16], ALU.subtract))
                        link(h, 3, e.tensor_copy(s.mparts[:, 16:32], s.mrest))
                        e.tensor_tensor(s.mparts[:, 32:48], s.mrest, s.mparts[:, 16:32], ALU.subtract).then_inc(s.maxrow_split, 1)
                elif x[0] == "maxrow":
                    e.tensor_copy(s.mrow[:, (b + 1) % 2, :], ps[0:48, 0:64].bitcast(BF16)).then_inc(s.maxrow_turned, 1)
                    e.wait_ge(s.maxrow_turned, h + 1)
                    e.sem_inc(s.ring_freed, 1)
                else:
                    c = x[1]
                    got = ps[:, 0:P].rearrange("p (t k) -> p t k", k=32)[:, :, 0:2 * (HD + 1)].rearrange("p t (g j) -> p t g j", g=2)
                    e.reciprocal(s.recip[:, c % 2, :, :], got[:, :, :, HD]).then_inc(s.recip_ready, 1)
                    e.wait_ge(s.recip_ready, NC * pair + c + 1)
                    e.tensor_tensor(tiled(s.ctx)[:, 4 * c:4 * c + 4, bass.ds(2 * pair * HD, 2 * HD)].rearrange("p t (g j) -> p t g j", g=2),
                                    got[:, :, :, 0:HD], s.recip[:, c % 2, :, :].unsqueeze(3).to_broadcast([P, 4, 2, HD]),
                                    ALU.mult).then_inc(s.ring_freed, 1)

            def add_context(pair, c):
                e.wait_ge(s.context_done, NP * (2 * pair + 1) + LAST[c] // 2 + 3)
                e.tensor_tensor(s.oe[:, c, :], s.oe[:, c, :], context_bank, ALU.add).then_inc(s.context_read, 1)

            def step(pair, b):
                idx = 0
                for x in order_of(pair, b):
                    if x[0] == "context" and b == 1 and 2 * x[1] + 1 in LAST:
                        add_context(pair, LAST.index(2 * x[1] + 1))
                    elif x[0] in ("max", "maxrow", "turn"):
                        ring_read(pair, b, ring(phase(pair, b) + idx), first_piece(pair, b) + idx, x)
                        idx += 1

            for n, x in enumerate(FIRST_RING):
                ring_read(-1, 1, ring(AHEAD + n), AHEAD + n, x)
            with e.Fori(0, PAIRS - 1) as i:
                step(i, 0)
                step(i, 1)
            step(PAIRS - 1, 0)
            step(PAIRS - 1, 1)
            e.wait_ge(s.out_filled, 1)
            finish(e, s)

        hidden = slot(0)
        hidden2 = slot(2)
        att0 = attention(0, slot(2), "ln_b1", w_att[0], None)
        h_biased = sem("h_biased")
        ln1_scaled = sem("ln1_scaled")
        hidden2_ready = sem("hidden2_ready")
        ATT_LOADS = 16

        def attention_loads(e):
            names = ("q", "k", "v", "o")
            for i, n in enumerate(names):
                e.dma_start(w_att[0][:, i, :], a[f"L0_ffn_{n}_w"]).then_inc(attention_weights_loaded, 16)
                e.dma_start(w_raw[:, i, :], a[f"L1_attn_W{n}"]).then_inc(attention_weights_loaded, 16)
            for dst, src in ((q_b, "q_b"), (k_b, "k_b")):
                e.dma_start(dst, a[f"L0_ffn_{src}"].rearrange("(p a) -> p a", a=1)).then_inc(attention_weights_loaded, 16)
            for dst, src in ((ln1_w, "ln1_w"), (ln1_b, "ln1_b"), (v_b_row, "v_b"), (o_b_row, "o_b"), (ln2_w, "ln2_w"), (ln2_b, "ln2_b")):
                e.dma_start(dst, row_of(a[f"L0_ffn_{src}"])).then_inc(attention_weights_loaded, 16)

        def wide(row):
            return row.unsqueeze(1).to_broadcast([P, NT, D])

        def att0_before_dve(e):
            norm_dve(e, "ln_b", x1, hidden)
            e.wait_ge(attention_weights_loaded, 16 * ATT_LOADS)
            e.tensor_scalar(q_b_scaled, q_b, SCORE_SCALE, None, ALU.mult)
            norm_dve(e, "ln_b1", hidden, att0.xn, affine=(ln1_w, ln1_b))

        def att0_before_pool(e):
            e.wait_ge(attention_weights_loaded, 16 * ATT_LOADS)
            e.wait_ge(tile_normed, normed("ln_b1"))
            e.tensor_tensor(tiled(hidden), tiled(hidden), wide(o_b_row), ALU.add).then_inc(h_biased, 1)
            e.wait_ge(h_biased, 1)

        def att0_finish(e, s):
            e.wait_ge(h_biased, 1)
            e.tensor_tensor(hidden2, psum_b[:, :], hidden, ALU.add).then_inc(hidden2_ready, 1)
            e.wait_ge(hidden2_ready, 1)

        def top_two(e, link, logits, picks, E, expert_ids, largest, second, spare, spare2, index):
            def wide_e(v):
                return v.unsqueeze(2).to_broadcast([P, NT, E])
            source = logits
            for k, value in enumerate((largest, second)):
                link(e, e.tensor_reduce(value, source, AX.X, ALU.max))
                link(e, e.tensor_tensor(spare, source, wide_e(value), ALU.is_equal))
                link(e, e.scalar_tensor_tensor(spare, spare, -64.0, expert_ids, ALU.mult, ALU.add))
                link(e, e.tensor_reduce(index, spare, AX.X, ALU.min))
                link(e, e.tensor_scalar(index, index, 64.0, None, ALU.add))
                link(e, e.tensor_tensor(picks[k], expert_ids, wide_e(index), ALU.is_equal))
                if k == 0:
                    link(e, e.scalar_tensor_tensor(spare2, picks[0], NEG, logits, ALU.mult, ALU.add))
                    source = spare2

        xt, xtT = slot(3), slot(4)
        fc1 = arena[:, 5, 0:2 * F0].rearrange("p (b f) -> p b f", b=2)
        fc2 = arena[:, 5, 2 * F0:4 * F0].rearrange("p (b k n) -> p b k n", b=2, n=D)
        KF = F0 // P
        ST = CAP // P
        x_exp = arena[:, 6, 0:2 * CAP].rearrange("p (b s d) -> p b s d", b=2, d=D)
        x_expT = arena[:, 6, 2 * CAP:4 * CAP].rearrange("p (b s) -> p b s", b=2)
        y_exp = arena[:, 6, 4 * CAP:6 * CAP].rearrange("p (b s d) -> p b s d", b=2, d=D)
        h_exp = arena[:, 7, :].rearrange("p (b k s) -> p b k s", b=2, k=KF)
        fc2_b = arena[0:1, 8, :]
        got = [slot(9), slot(10)]
        fc1_b_raw = arena[0:E0 * KF, 11, 0:P]
        fc1_b = arena[:, 11, P:P + E0 * KF]
        router_w = arena[:, 11, 256:256 + E0]
        small = arena[:, 12:14, :].rearrange("p a n -> p (a n)")

        def cut(at, n):
            return small[:, at:at + n]

        def by_expert(v, E=E0):
            return v.rearrange("p (t e) -> p t e", e=E)
        logits, expert_ids, spare, spare2, probs = (by_expert(cut(256 * i, 256)) for i in range(5))
        picks = cut(1280, 512).rearrange("p (t s e) -> p t s e", s=2, e=E0)
        picks_bf = cut(1792, 256).bitcast(BF16)
        place = cut(2048, 512).rearrange("p (t s e) -> p t s e", s=2, e=E0)
        before = cut(2560, 512).rearrange("p (t s e) -> p t s e", s=2, e=E0)
        largest, second, index, total, = (cut(3072 + 16 * i, 16) for i in range(4))
        slot_of, kept, gates, dump_row, to_scatter, to_gather = (cut(3136 + 32 * i, 32).rearrange("p (t s) -> p t s", s=2) for i in range(6))
        ids_int = cut(3328, 256).bitcast(I32)
        dump_int = cut(3584, 32).bitcast(I32)
        scatter_int, gather_int = (cut(3616 + 32 * i, 32).bitcast(I32) for i in range(2))
        zeros = sb("zeros", [P, 1024])

        DUMP = SLOTS
        xin_dram = nc.dram_tensor("expert_inputs", [SLOTS + 2 * T, D], F32).ap()
        eout_dram = nc.dram_tensor("expert_outputs", [SLOTS + P, D], F32).ap()

        zeros_set, dram_zeroed = sem("zeros_set"), sem("dram_zeroed")
        moe_loaded = sem("moe_loaded")
        xtT_filled, xtT_read = sem("xtT_filled"), sem("xtT_read")
        logits_filled, picks_ready, places_filled, routed = sem("logits_filled"), sem("picks_ready"), sem("places_filled"), sem("routed")
        moe_iota, fc1_b_read = sem("moe_iota"), sem("fc1_b_read")
        shifted_ready, exp_ready = sem("shifted_ready"), sem("exp_ready")
        scattered, gathered = sem("scattered"), [sem(f"gathered{c}") for c in range(NC)]
        fc_loaded = [sem(f"fc_loaded{b}") for b in range(2)]
        x_exp_loaded = [sem(f"x_exp_loaded{b}") for b in range(2)]
        x_exp_turned, x_exp_read, h_filled, h_ready, y_filled, y_exp_ready = (
            sem(n) for n in ("x_exp_turned", "x_exp_read", "h_filled", "h_ready", "y_filled", "y_exp_ready"))
        y_exp_stored = [sem(f"y_exp_stored{b}") for b in range(2)]
        x12_ready = sem("x12_ready")
        combined = sem("combined")
        x2 = slot(1)

        def moe0_zero(e):
            e.wait_ge(zeros_set, 1)
            rows_each = 1024 // D
            for i in range(SLOTS // (P * rows_each)):
                e.dma_start(xin_dram[i * P * rows_each:(i + 1) * P * rows_each, :].rearrange("(p r) d -> p (r d)", p=P),
                            zeros[:, :]).then_inc(dram_zeroed, 16)
            e.dma_start(eout_dram[SLOTS:SLOTS + P, :], zeros[:, 0:D]).then_inc(dram_zeroed, 16)
        ZEROED = 16 * (SLOTS // (P * 8) + 1)

        def moe0_sync(e):
            e.wait_ge(hidden2_ready, 1)
            e.dma_start(fc2_b, a["L0_ffn_fc2_b"].rearrange("(a e) n -> a (e n)", a=1)).then_inc(moe_loaded, 16)
            e.dma_start(fc1_b_raw, a["L0_ffn_fc1_b"].rearrange("e (k p) -> (e k) p", p=P)).then_inc(moe_loaded, 16)
            e.dma_start(router_w, a["L0_ffn_router_w"]).then_inc(moe_loaded, 16)

            def weights(x, b):
                e.dma_start(fc1[:, b, :], a["L0_ffn_fc1_w"][bass.ds(x, 1), :, :].rearrange("a d f -> (a d) f")).then_inc(fc_loaded[b], 16)
                e.dma_start(fc2[:, b, :, :], a["L0_ffn_fc2_w"][bass.ds(x, 1), :, :].rearrange("a (k p) n -> p (a k) n", p=P)).then_inc(fc_loaded[b], 16)

            def inputs(x, b):
                e.dma_start(x_exp[:, b, :, :], xin_dram[bass.ds(x * CAP, CAP), :].rearrange("(s p) d -> p s d", p=P)).then_inc(x_exp_loaded[b], 16)

            def store(x, b):
                e.wait_ge(y_exp_ready, x + 1)
                e.dma_start(eout_dram[bass.ds(x * CAP, CAP), :].rearrange("(s p) d -> p s d", p=P), y_exp[:, b, :, :]).then_inc(y_exp_stored[b], 16)

            for b in range(2):
                weights(b, b)
            e.wait_ge(scattered, 16 * 2 * NT)
            for b in range(2):
                inputs(b, b)

            def follow(x, b, more=True):
                if more:
                    e.wait_ge(x_exp_read, x + 1)
                    inputs(x + 2, b)
                store(x, b)
                if more:
                    weights(x + 2, b)
            with e.Fori(0, E0 // 2 - 1) as i:
                follow(2 * i, 0)
                follow(2 * i + 1, 1)
            follow(E0 - 2, 0, more=False)
            follow(E0 - 1, 1, more=False)

        def moe0_pool(e):
            e.wait_ge(hidden2_ready, 1)
            e.tensor_tensor(x2, x1, hidden2, ALU.add).then_inc(x12_ready, 1)
            e.wait_ge(x12_ready, 1)
            e.iota(ids_int, pattern=[[0, NT], [1, E0]], base=0, channel_multiplier=0).then_inc(moe_iota, 1)
            e.iota(dump_int, pattern=[[P, NT], [T, 2]], base=DUMP, channel_multiplier=1).then_inc(moe_iota, 1)
            e.wait_ge(routed, 1)
            e.wait_ge(dram_zeroed, ZEROED)
            for t in range(NT):
                for k in range(2):
                    e.indirect_dma_start(out=xin_dram, out_offset=bass.IndirectOffsetOnAxis(ap=scatter_int[:, 2 * t + k:2 * t + k + 1], axis=0),
                                         in_=xt[:, t * D:(t + 1) * D], in_offset=None).then_inc(scattered, 16)
            for b in range(2):
                e.wait_ge(y_exp_stored[b], 16 * E0 // 2)
            for t in range(NT):
                for k in range(2):
                    e.indirect_dma_start(out=got[k][:, t * D:(t + 1) * D], out_offset=None, in_=eout_dram,
                                         in_offset=bass.IndirectOffsetOnAxis(ap=gather_int[:, 2 * t + k:2 * t + k + 1], axis=0)).then_inc(gathered[t // 4], 16)

        def moe0_pe(e):
            turn_normed(e, "ln_b2", xt, xtT_filled)
            e.wait_ge(moe_loaded, 48)
            e.transpose(psum_b[:, CW:CW + E0 * KF], fc1_b_raw, ident[0:E0 * KF, 0:E0 * KF])
            for t in range(NT):
                if t % 4 == 0:
                    e.wait_ge(xtT_read, t // 4 + 1)
                i = e.matmul(psum_b[:, t * E0:(t + 1) * E0], xtT[:, t * P:(t + 1) * P], router_w, start=True, stop=True)
            i.then_inc(logits_filled, 1)
            e.wait_ge(picks_ready, 1)
            e.matmul(psum_a[:, 0:CW], tri_bf[:, :], picks_bf, start=True, stop=True)
            e.matmul(psum_a[:, CW:2 * CW], ones_bf[:, :], picks_bf, start=True, stop=True).then_inc(places_filled, 1)
            e.wait_ge(routed, 1)

            def up(x, pair, b, first=False):
                ps = psum_ab[b]
                e.wait_ge(x_exp_loaded[b], 16 * (pair + 1))
                for s in range(ST):
                    i = e.transpose(ps[:, s * P:(s + 1) * P], x_exp[:, b, s, :], ident[:, :])
                i.then_inc(x_exp_turned, 1)
                e.wait_ge(fc_loaded[b], 32 * (pair + 1))
                e.wait_ge(x_exp_read, x + 1)
                for k in range(KF):
                    i = e.matmul(ps[:, CW + k * CAP:CW + (k + 1) * CAP], fc1[:, b, k * P:(k + 1) * P], x_expT[:, b, :], start=True, stop=True)
                i.then_inc(h_filled, 1)

            def down(x, b):
                ps = psum_ab[b]
                e.wait_ge(h_ready, x + 1)
                for s in range(ST):
                    o = ps[:, 3 * CW + s * P:3 * CW + (s + 1) * P]
                    e.matmul(o, ones_row[:, :], fc2_b[:, ds(x, D)], start=True, stop=False)
                    for k in range(KF):
                        i = e.matmul(o, h_exp[:, b, k, s * P:(s + 1) * P], fc2[:, b, k, :], start=False, stop=(k == KF - 1))
                i.then_inc(y_filled, 1)

            with e.Fori(0, E0 // 2) as i:
                up(2 * i, i, 0)
                up(2 * i + 1, i, 1)
                down(2 * i, 0)
                down(2 * i + 1, 1)

        def moe0_act(e):
            norm_act(e, "ln_b2")
            read_turned(e, xtT, xtT_filled, xtT_read)
            e.wait_ge(logits_filled, 1)
            e.activation(fc1_b, psum_b[:, CW:CW + E0 * KF], ACT.Copy).then_inc(fc1_b_read, 1)
            e.wait_ge(shifted_ready, 1)
            e.activation(probs, probs, ACT.Exp).then_inc(exp_ready, 1)
            e.wait_ge(fc1_b_read, 1)

            def hidden_units(x, b):
                e.wait_ge(h_filled, x + 1)
                for k in range(KF):
                    i = e.activation(h_exp[:, b, k, :], psum_ab[b][:, CW + k * CAP:CW + (k + 1) * CAP], ACT.Gelu,
                                     bias=fc1_b[:, bass.ds(x * KF + k, 1)])
                i.then_inc(h_ready, 1)
            with e.Fori(0, E0 // 2) as i:
                hidden_units(2 * i, 0)
                hidden_units(2 * i + 1, 1)

        def moe0_dve(e):
            norm_dve(e, "ln_b2", hidden2, xt, affine=(ln2_w, ln2_b))
            e.wait_ge(moe_iota, 2)
            dve_link(e, e.tensor_copy(expert_ids, by_expert(ids_int)))
            dve_link(e, e.tensor_copy(dump_row, dump_int.rearrange("p (t s) -> p t s", s=2)))
            e.wait_ge(logits_filled, 1)
            dve_link(e, e.tensor_copy(logits, by_expert(psum_b[:, 0:NT * E0])))
            top_two(e, dve_link, logits, [picks[:, :, k, :] for k in range(2)], E0, expert_ids, largest, second, spare, spare2, index)
            e.tensor_copy(picks_bf, picks.rearrange("p t s e -> p (t s e)")).then_inc(picks_ready, 1)

            def wide_e(v):
                return v.unsqueeze(2).to_broadcast([P, NT, E0])
            e.tensor_tensor(probs, logits, wide_e(largest), ALU.subtract).then_inc(shifted_ready, 1)
            inclusive = psum_a[:, 0:CW].rearrange("p (t s e) -> p t s e", s=2, e=E0)
            totals = psum_a[:, CW:2 * CW].rearrange("p (t s e) -> p t s e", s=2, e=E0)
            dve_link(e, e.memset(before[:, 0, :, :], 0.0))
            e.wait_ge(places_filled, 1)
            for t in range(1, NT):
                dve_link(e, e.tensor_tensor(before[:, t, :, :], totals[:, t - 1, :, :], before[:, t - 1, :, :], ALU.add))
            dve_link(e, e.tensor_tensor(total, totals[:, NT - 1, 0, :], before[:, NT - 1, 0, :], ALU.add))
            dve_link(e, e.tensor_tensor(place, inclusive, before, ALU.add))
            dve_link(e, e.tensor_tensor(place[:, :, 1, :], place[:, :, 1, :], total.unsqueeze(1).to_broadcast([P, NT, E0]), ALU.add))
            flat = [v.rearrange("p t s e -> p (t s e)") for v in (place, picks)]
            dve_link(e, e.scalar_tensor_tensor(flat[1], flat[0], CAP + 0.5, flat[1], ALU.is_lt, ALU.mult))
            dve_link(e, e.tensor_reduce(kept, picks, AX.X, ALU.add))
            for k in range(2):
                dve_link(e, e.scalar_tensor_tensor(spare, expert_ids, float(CAP), place[:, :, k, :], ALU.mult, ALU.add))
                dve_link(e, e.scalar_tensor_tensor(spare, spare, -1.0, picks[:, :, k, :], ALU.add, ALU.mult))
                dve_link(e, e.tensor_reduce(slot_of[:, :, k], spare, AX.X, ALU.add))
            dve_link(e, e.tensor_tensor(to_scatter, kept, dump_row, ALU.mult))
            dve_link(e, e.tensor_tensor(to_scatter, dump_row, to_scatter, ALU.subtract))
            dve_link(e, e.tensor_tensor(to_scatter, to_scatter, slot_of, ALU.add))
            dve_link(e, e.tensor_scalar(to_gather, kept, -float(SLOTS), float(SLOTS), ALU.mult, ALU.add))
            dve_link(e, e.tensor_tensor(to_gather, to_gather, slot_of, ALU.add))
            dve_link(e, e.tensor_copy(gather_int, to_gather.rearrange("p t s -> p (t s)")))
            e.tensor_copy(scatter_int, to_scatter.rearrange("p t s -> p (t s)")).then_inc(routed, 1)
            e.wait_ge(exp_ready, 1)
            dve_link(e, e.tensor_reduce(index, probs, AX.X, ALU.add))
            dve_link(e, e.reciprocal(index, index))
            dve_link(e, e.tensor_tensor(probs, probs, wide_e(index), ALU.mult))
            for k in range(2):
                dve_link(e, e.tensor_tensor(spare, probs, picks[:, :, k, :], ALU.mult))
                dve_link(e, e.tensor_reduce(gates[:, :, k], spare, AX.X, ALU.add))
            dve_link(e, e.tensor_tensor(index, gates[:, :, 0], gates[:, :, 1], ALU.add))
            dve_link(e, e.tensor_scalar(index, index, 1.1920929e-07, None, ALU.max))
            dve_link(e, e.reciprocal(index, index))
            for k in range(2):
                dve_link(e, e.tensor_tensor(gates[:, :, k], gates[:, :, k], index, ALU.mult))

            def expert(x, pair, b):
                ps = psum_ab[b]
                e.wait_ge(x_exp_turned, x + 1)
                e.tensor_copy(x_expT[:, b, :], ps[:, 0:CAP]).then_inc(x_exp_read, 1)

            def outputs(x, pair, b, first=False):
                e.wait_ge(y_filled, x + 1)
                if not first:
                    e.wait_ge(y_exp_stored[b], 16 * pair)
                e.tensor_scalar(y_exp[:, b, :, :], psum_ab[b][:, 3 * CW:3 * CW + CAP].rearrange("p (s d) -> p s d", d=D),
                                1.0 - 0.2, None, ALU.mult).then_inc(y_exp_ready, 1)

            def both(i, first=False):
                expert(2 * i, i, 0)
                expert(2 * i + 1, i, 1)
                outputs(2 * i, i, 0, first)
                outputs(2 * i + 1, i, 1, first)
            both(0, first=True)
            with e.Fori(1, E0 // 2) as i:
                both(i)
            for c in range(NC):
                e.wait_ge(gathered[c], 16 * 2 * 4)
                for k in range(2):
                    for t in range(4 * c, 4 * c + 4):
                        i = e.scalar_tensor_tensor(x2[:, t * D:(t + 1) * D], got[k][:, t * D:(t + 1) * D], gates[:, t, k:k + 1],
                                                   x2[:, t * D:(t + 1) * D], ALU.mult, ALU.add)
                    i.then_inc(combined, 1)
                    e.wait_ge(combined, 2 * c + k + 1)

        x3 = slot(0)
        att1 = attention(1, slot(2), "ln_c", w_att[1], w_raw)
        x3_ready = sem("x3_ready")

        def att1_before_dve(e):
            norm_dve(e, "ln_c", x2, att1.xn)

        def att1_finish(e, s):
            e.tensor_tensor(x3, psum_b[:, :], x2, ALU.add).then_inc(x3_ready, 1)
            e.wait_ge(x3_ready, 1)

        xf, xfT = slot(2), slot(3)
        KH = F1 // P
        w_gate = arena[:, 5, 0:2 * F1].rearrange("p (b f) -> p b f", b=2)
        w_up = arena[:, 5, 2 * F1:4 * F1].rearrange("p (b f) -> p b f", b=2)
        w_down = arena[:, 5, 4 * F1:4 * F1 + 2 * KH * D].rearrange("p (b k n) -> p b k n", b=2, n=D)
        silu_g = arena[:, 6, :].rearrange("p (b n) -> p b n", b=2)
        prod = arena[:, 7, :].rearrange("p (b k n) -> p b k n", b=2, k=KH)
        router1_raw = arena[0:E1, 11, 0:P]
        router1_w = arena[:, 11, P:P + E1]
        router1_b = arena[:, 11, 2 * P:2 * P + E1]
        logits1, ids1, spare1, spare1b = (cut(128 * i, 128).rearrange("p (t e) -> p t e", e=E1) for i in range(4))
        picks1 = cut(512, 256).rearrange("p (s t e) -> p s t e", s=2, e=E1)
        weight1 = cut(768, NT * (E1 + 1)).rearrange("p (t e) -> p t e", e=E1 + 1)
        largest1, second1, index1, share1 = (cut(1024 + 16 * i, 16) for i in range(4))
        ids1_int = cut(1152, 128).bitcast(I32).rearrange("p (t e) -> p t e", e=E1)
        UNITS = (E1 + 1) * NC

        moe1_loaded, moe1_iota = sem("moe1_loaded"), sem("moe1_iota")
        xfT_filled, xfT_read = sem("xfT_filled"), sem("xfT_read")
        router1_turned, router1_read, logits1_filled = sem("router1_turned"), sem("router1_read"), sem("logits1_filled")
        gap_ready, gap_exp, weights1_ready = sem("gap_ready"), sem("gap_exp"), sem("weights1_ready")
        expert_loaded = [sem(f"expert_loaded{b}") for b in range(2)]
        units_filled, silu_ready, prod_ready, down_filled, unit_added = (
            sem(n) for n in ("units_filled", "silu_ready", "prod_ready", "down_filled", "unit_added"))

        def moe1_sync(e):
            e.wait_ge(x3_ready, 1)
            e.dma_start(router1_raw, a["L1_ffn_router_w"]).then_inc(moe1_loaded, 16)
            e.dma_start(router1_b, row_of(a["L1_ffn_experts_bias"])).then_inc(moe1_loaded, 16)

            def weights(names, x, b):
                gate, up, down = (a[f"L1_ffn_{n}"][bass.ds(x, 1), :, :] for n in names)
                e.dma_start(w_gate[:, b, :], gate.rearrange("a d f -> (a d) f")).then_inc(expert_loaded[b], 16)
                e.dma_start(w_up[:, b, :], up.rearrange("a d f -> (a d) f")).then_inc(expert_loaded[b], 16)
                e.dma_start(w_down[:, b, :, :], down.rearrange("a (k p) n -> p (a k) n", p=P)).then_inc(expert_loaded[b], 16)
            routed_names = ("w1", "w3", "w2")
            weights(routed_names, 0, 0)
            weights(routed_names, 1, 1)
            with e.Fori(0, E1 // 2 - 1) as i:
                for b in range(2):
                    e.wait_ge(down_filled, NC * (2 * i + b + 1))
                    weights(routed_names, 2 * i + b + 2, b)
            e.wait_ge(down_filled, NC * (E1 - 1))
            weights(("sw1", "sw3", "sw2"), 0, 0)

        def moe1_pool(e):
            e.wait_ge(x3_ready, 1)
            e.iota(ids1_int, pattern=[[0, NT], [1, E1]], base=0, channel_multiplier=0).then_inc(moe1_iota, 1)

        def moe1_pe(e):
            turn_normed(e, "ln_d", xf, xfT_filled)
            e.wait_ge(moe1_loaded, 32)
            e.transpose(psum_b[:, CW:CW + E1], router1_raw, ident[0:E1, 0:E1]).then_inc(router1_turned, 1)
            e.wait_ge(router1_read, 1)
            for t in range(NT):
                if t % 4 == 0:
                    e.wait_ge(xfT_read, t // 4 + 1)
                i = e.matmul(psum_b[:, t * E1:(t + 1) * E1], xfT[:, t * P:(t + 1) * P], router1_w, start=True, stop=True)
            i.then_inc(logits1_filled, 1)

            def gate_up(c, b, u, first):
                ps = psum_ab[c % 2]
                for m, w, k in ((1, w_up, 0), (1, w_up, 1), (0, w_gate, 1), (0, w_gate, 0)):
                    if (m, k) == (0, 0) and not first:
                        e.wait_ge(unit_added, u - 1)
                    i = e.matmul(ps[:, (KH * m + k) * CW:(KH * m + k + 1) * CW], w[:, b, k * P:(k + 1) * P],
                                 xfT[:, c * CW:(c + 1) * CW], start=True, stop=True)
                i.then_inc(units_filled, 1)

            def down(c, b, u):
                e.wait_ge(prod_ready, u + 1)
                for t in range(4):
                    for k in range(KH):
                        i = e.matmul(psum_ab[c % 2][:, t * P:(t + 1) * P], prod[:, c % 2, k, t * P:(t + 1) * P], w_down[:, b, k, :],
                                     start=(k == 0), stop=(k == KH - 1))
                i.then_inc(down_filled, 1)

            def next_unit(c, b, u, first=False):
                if c == 0:
                    e.wait_ge(expert_loaded[b], 48 * (next_unit.pair + 1))
                gate_up(c, b, u, first)

            e.wait_ge(weights1_ready, 1)
            next_unit.pair = 0
            next_unit(0, 0, 0, first=True)
            next_unit(1, 0, 1, first=True)
            down(0, 0, 0)
            next_unit(2, 0, 2)
            down(1, 0, 1)
            next_unit(3, 0, 3)
            down(2, 0, 2)
            next_unit.pair = 0
            next_unit(0, 1, 4)
            down(3, 0, 3)

            def expert_units(x, b, pair, nxt):
                for c in range(1, NC):
                    next_unit(c, b, NC * x + c)
                    down(c - 1, b, NC * x + c - 1)
                next_unit.pair = nxt
                next_unit(0, 1 - b, NC * (x + 1))
                down(NC - 1, b, NC * x + NC - 1)

            expert_units(1, 1, 0, 1)
            with e.Fori(1, E1 // 2) as i:
                expert_units(2 * i, 0, i, i)
                expert_units(2 * i + 1, 1, i, i + 1)
            for c in range(1, NC):
                next_unit(c, 0, NC * E1 + c)
                down(c - 1, 0, NC * E1 + c - 1)
            down(NC - 1, 0, UNITS - 1)

        def moe1_act(e):
            norm_act(e, "ln_d")
            read_turned(e, xfT, xfT_filled, xfT_read)
            e.wait_ge(router1_turned, 1)
            e.activation(router1_w, psum_b[:, CW:CW + E1], ACT.Copy).then_inc(router1_read, 1)
            e.wait_ge(gap_ready, 1)
            e.activation(share1, share1, ACT.Exp).then_inc(gap_exp, 1)

            def unit(c, u, first=False):
                e.wait_ge(units_filled, u + 1)
                if not first:
                    e.wait_ge(prod_ready, u - 1)
                e.activation(silu_g[:, c % 2, :], psum_ab[c % 2][:, 0:KH * CW], ACT.Silu).then_inc(silu_ready, 1)
            for c in range(NC):
                unit(c, c, first=(c < 2))
            with e.Fori(1, E1 + 1) as x:
                for c in range(NC):
                    unit(c, NC * x + c)

        def moe1_dve(e):
            norm_dve(e, "ln_d", x3, xf)
            e.wait_ge(moe1_iota, 1)
            dve_link(e, e.tensor_copy(ids1, ids1_int))
            e.wait_ge(logits1_filled, 1)
            dve_link(e, e.tensor_tensor(logits1, psum_b[:, 0:NT * E1].rearrange("p (t e) -> p t e", e=E1),
                                        router1_b.unsqueeze(1).to_broadcast([P, NT, E1]), ALU.add))
            top_two(e, dve_link, logits1, [picks1[:, k, :, :] for k in range(2)], E1, ids1, largest1, second1, spare1, spare1b, index1)
            e.tensor_tensor(share1, second1, largest1, ALU.subtract).then_inc(gap_ready, 1)
            e.wait_ge(gap_exp, 1)
            dve_link(e, e.tensor_scalar(largest1, share1, 1.0, None, ALU.add))
            dve_link(e, e.reciprocal(largest1, largest1))
            dve_link(e, e.tensor_tensor(share1, share1, largest1, ALU.mult))

            def wide_e(v):
                return v.unsqueeze(2).to_broadcast([P, NT, E1])
            dve_link(e, e.tensor_tensor(spare1, picks1[:, 0, :, :], wide_e(largest1), ALU.mult))
            dve_link(e, e.tensor_tensor(spare1b, picks1[:, 1, :, :], wide_e(share1), ALU.mult))
            dve_link(e, e.memset(weight1, 1.0))
            e.tensor_tensor(weight1[:, :, 0:E1], spare1, spare1b, ALU.add).then_inc(weights1_ready, 1)
            e.wait_ge(weights1_ready, 1)

            def product(c, u, first=False):
                e.wait_ge(silu_ready, u + 1)
                if not first:
                    e.wait_ge(down_filled, u - 1)
                e.tensor_tensor(prod[:, c % 2, :, :].rearrange("p k n -> p (k n)"), silu_g[:, c % 2, :],
                                psum_ab[c % 2][:, KH * CW:2 * KH * CW], ALU.mult).then_inc(prod_ready, 1)

            def add(c, x, u):
                e.wait_ge(down_filled, u + 1)
                for k in range(4):
                    t = 4 * c + k
                    i = e.scalar_tensor_tensor(x3[:, t * D:(t + 1) * D], psum_ab[c % 2][:, k * P:(k + 1) * P],
                                               weight1[:, t, bass.ds(x, 1)], x3[:, t * D:(t + 1) * D], ALU.mult, ALU.add)
                i.then_inc(unit_added, 1)

            product(0, 0, first=True)
            for c in range(1, NC):
                product(c, c, first=(c < 2))
                add(c - 1, 0, c - 1)
            with e.Fori(1, E1 + 1) as x:
                product(0, NC * x)
                add(NC - 1, x - 1, NC * x - 1)
                for c in range(1, NC):
                    product(c, NC * x + c)
                    add(c - 1, x, NC * x + c - 1)
            add(NC - 1, E1, UNITS - 1)

        out_stored = sem("out_stored")
        block = ctx.enter_context(nc.Block())

        @block.sync
        def _(e):
            mamba_loads(e)
            moe0_zero(e)
            attention_loads(e)
            att_sync(e, att0)
            moe0_sync(e)
            att_sync(e, att1)
            moe1_sync(e)
            for c in range(NC):
                e.wait_ge(unit_added, UNITS - NC + c + 1)
                e.dma_start(out.rearrange("b (t p) d -> p (b t) d", p=P)[:, 4 * c:4 * c + 4, :],
                            tiled(x3)[:, 4 * c:4 * c + 4, :]).then_inc(out_stored, 16)
            e.wait_ge(out_stored, 16 * NC)
            e.wait_ge(dram_zeroed, ZEROED)

        @block.gpsimd
        def _(e):
            e.memset(zeros[:, :], 0.0).then_inc(zeros_set, 1)
            constants_pool(e)
            mamba_pool(e)
            att0_before_pool(e)
            att_pool(e, att0)
            moe0_pool(e)
            att_pool(e, att1)
            moe1_pool(e)

        @block.scalar
        def _(e):
            mamba_act(e)
            norm_act(e, 'ln_b')
            norm_act(e, 'ln_b1')
            att_act(e, att0)
            moe0_act(e)
            norm_act(e, 'ln_c')
            att_act(e, att1)
            moe1_act(e)

        @block.vector
        def _(e):
            mamba_dve(e)
            att0_before_dve(e)
            att_dve(e, att0, att0_finish)
            moe0_dve(e)
            att1_before_dve(e)
            att_dve(e, att1, att1_finish)
            moe1_dve(e)

        @block.tensor
        def _(e):
            mamba_pe(e)
            att_pe(e, att0)
            moe0_pe(e)
            att_pe(e, att1)
            moe1_pe(e)


_INS = [
    'L0_attn_x', 'L0_attn_W_in_o', 'L0_attn_b_in_o', 'L0_attn_W_out_o', 'L0_attn_b_out_o', 'L0_attn_W_in_i',
    'L0_attn_conv_w', 'L0_attn_conv_b', 'L0_attn_W_xp', 'L0_attn_W_dt', 'L0_attn_b_dt', 'L0_attn_A_log',
    'L0_attn_D_skip', 'L0_attn_W_out_i', 'L0_ffn_ln1_w', 'L0_ffn_ln1_b', 'L0_ffn_q_w', 'L0_ffn_q_b',
    'L0_ffn_k_w', 'L0_ffn_k_b', 'L0_ffn_v_w', 'L0_ffn_v_b', 'L0_ffn_o_w', 'L0_ffn_o_b', 'L0_ffn_ln2_w',
    'L0_ffn_ln2_b', 'L0_ffn_router_w', 'L0_ffn_fc1_w', 'L0_ffn_fc1_b', 'L0_ffn_fc2_w', 'L0_ffn_fc2_b',
    'L1_attn_Wq', 'L1_attn_Wk', 'L1_attn_Wv', 'L1_attn_Wo', 'L1_ffn_router_w', 'L1_ffn_experts_bias',
    'L1_ffn_w1', 'L1_ffn_w3', 'L1_ffn_w2', 'L1_ffn_sw1', 'L1_ffn_sw3', 'L1_ffn_sw2'
]
_OUTS = [((1, 2048, 128), 'float32')]


def kernel(**inputs):
    import numpy as _np
    import concourse.bacc as _bacc
    from concourse import mybir as _mybir
    from concourse.bass_utils import run_bass_kernel_spmd as _run

    nc = _bacc.Bacc("TRN2", target_bir_lowering=False, num_devices=1)
    arrays, args = {}, {}
    for name in _INS:
        v = _np.ascontiguousarray(inputs[name])
        arrays[f"in_{name}_dram"] = v
        args[name] = nc.dram_tensor(f"in_{name}_dram", v.shape, _mybir.dt.from_np(v.dtype), kind="ExternalInput").ap()
    shape, dtype = _OUTS[0]
    out = nc.dram_tensor("out_0_dram", shape, _mybir.dt.from_np(_np.dtype(dtype)), kind="ExternalOutput").ap()
    program(nc, args, out)
    r = _run(nc, [arrays], core_ids=[0])
    return r.results[0]["out_0_dram"]
```
